# Optimizing a Trainium2 kernel written in Bass

```python
import numpy as np
import jax
import jax.numpy as jnp

def _softmax(x, axis=-1):
    return jax.nn.softmax(x, axis=axis)
def _gelu(x):
    return jax.nn.gelu(x, approximate=True)
def _silu(x):
    return jax.nn.silu(x)
def _sigmoid(x):
    return jax.nn.sigmoid(x)
def _layernorm(x, axis=-1, eps=1e-5):
    m = jnp.mean(x, axis=axis, keepdims=True)
    v = jnp.var(x, axis=axis, keepdims=True)
    return (x - m) / jnp.sqrt(v + eps)
def _scatter_add(tgt, idx, src, axis=0):
    return tgt.at[idx].add(src)
def _segment_sum(src, seg, n):
    return jax.ops.segment_sum(src, seg, n)

kernel_name = 'mk_conv_seq_d2_conv_nchw128_03a95c'

def setup_inputs(seed: int = 0):
    np.random.seed(seed)
    _w = jnp.asarray
    def _rec_inputs():
        import jax
        import jax.numpy as jnp
        _gk = jax.random.key(seed)
        x = -0.0003929 + 0.9999 * jax.random.normal(jax.random.fold_in(_gk, 1), (32, 128, 64, 64), jnp.float32)
        return x
    x = _rec_inputs()
    def _L0_conv_setup():
        import jax, jax.numpy as jnp
        import numpy as np
        BN_EPS = 1e-05
        LN_EPS = 1e-06
        key = jax.random.key(seed)
        ks = jax.random.split(key, 8)
        B, C, H, W = (32, 128, 64, 64)
        A, K, KS = (16, 4, 3)
        s = lambda k, shape, sc=0.05: jax.random.normal(k, shape, jnp.float32) * sc
        return dict(x=jax.random.normal(ks[0], (B, C, H, W), jnp.float32), od_weight=s(ks[1], (K, C, 1, KS, KS), 0.1), fc_w=s(ks[2], (A, C)), bn_gamma=jnp.ones((A,), jnp.float32), bn_beta=jnp.zeros((A,), jnp.float32), bn_mean=jnp.zeros((A,), jnp.float32), bn_var=jnp.ones((A,), jnp.float32), ch_w=s(ks[3], (C, A)), ch_b=jnp.zeros((C,), jnp.float32), sp_w=s(ks[4], (KS * KS, A)), sp_b=jnp.zeros((KS * KS,), jnp.float32), ke_w=s(ks[5], (K, A)), ke_b=jnp.zeros((K,), jnp.float32), b1_w=s(ks[6], (C, C)), b1_b=jnp.zeros((C,), jnp.float32), b2_w=s(ks[7], (C, C)), b2_b=jnp.zeros((C,), jnp.float32), ln_w=jnp.ones((C,), jnp.float32), ln_b=jnp.zeros((C,), jnp.float32))
    _L0_conv_all = _L0_conv_setup()
    _L0_conv_in = {k: v for k, v in _L0_conv_all.items() if k in ('od_weight', 'fc_w', 'bn_gamma', 'bn_beta', 'bn_mean', 'bn_var', 'ch_w', 'ch_b', 'sp_w', 'sp_b', 'ke_w', 'ke_b', 'b1_w', 'b1_b', 'b2_w', 'b2_b', 'ln_w', 'ln_b', )}
    del _L0_conv_all

    def _L1_conv_setup():
        import jax, jax.numpy as jnp
        import numpy as np
        D_MODEL = 128
        D_STATE = 16
        D_CONV = 2
        EXPAND = 2
        D_INNER = EXPAND * D_MODEL
        DT_RANK = (D_MODEL + 15) // 16
        GROUPS = 4
        EPS = 1e-05

        def _causal_conv_k2(x, w, b):
            xp = jnp.pad(x, ((0, 0), (1, 0), (0, 0)))
            return xp[:, :-1] * w[:, 0] + xp[:, 1:] * w[:, 1] + b

        def _selective_scan(xc, dt, Bmat, Cmat, A, D):

            def step(h, inp):
                dt_t, B_t, C_t, x_t = inp
                dA = jnp.exp(dt_t[..., None] * A)
                dBx = dt_t[..., None] * B_t[:, None, :] * x_t[..., None]
                h = dA * h + dBx
                y = jnp.einsum('bdn,bn->bd', h, C_t)
                return (h, y)
            B_, L, Din = xc.shape
            h0 = jnp.zeros((B_, Din, A.shape[1]), dtype=xc.dtype)
            xs = (jnp.swapaxes(dt, 0, 1), jnp.swapaxes(Bmat, 0, 1), jnp.swapaxes(Cmat, 0, 1), jnp.swapaxes(xc, 0, 1))
            _, ys = jax.lax.scan(step, h0, xs)
            return jnp.swapaxes(ys, 0, 1) + xc * D

        def _mamba(x, W_in, conv_w, conv_b, W_x, W_dt, b_dt, A_log, D, W_out):
            xz = x @ W_in
            xh, z = jnp.split(xz, 2, axis=-1)
            xh = jax.nn.silu(_causal_conv_k2(xh, conv_w, conv_b))
            x_dbl = xh @ W_x
            dt_low = x_dbl[..., :DT_RANK]
            Bmat = x_dbl[..., DT_RANK:DT_RANK + D_STATE]
            Cmat = x_dbl[..., DT_RANK + D_STATE:]
            dt = jax.nn.softplus(dt_low @ W_dt + b_dt)
            A = -jnp.exp(A_log)
            y = _selective_scan(xh, dt, Bmat, Cmat, A, D)
            y = y * jax.nn.silu(z)
            return y @ W_out

        def _group_norm(x, gamma, beta):
            B_, C, H, W = x.shape
            xr = x.reshape(B_, GROUPS, -1)
            mean = xr.mean(-1, keepdims=True)
            var = xr.var(-1, keepdims=True)
            xn = ((xr - mean) * jax.lax.rsqrt(var + EPS)).reshape(B_, C, H, W)
            return xn * gamma[:, None, None] + beta[:, None, None]
        key = jax.random.key(seed)
        ks = jax.random.split(key, 12)
        s = lambda k, shape, sc=0.02: jax.random.normal(k, shape, dtype=jnp.float32) * sc
        inp = {'x_hsi': jax.random.normal(ks[0], (8, D_MODEL, 64, 64), dtype=jnp.float32), 'W_in': s(ks[1], (D_MODEL, 2 * D_INNER)), 'conv_w': s(ks[2], (D_INNER, D_CONV), 0.5), 'conv_b': s(ks[3], (D_INNER,), 0.1), 'W_x': s(ks[4], (D_INNER, DT_RANK + 2 * D_STATE)), 'W_dt': s(ks[5], (DT_RANK, D_INNER), 0.1), 'b_dt': s(ks[6], (D_INNER,), 0.1), 'A_log': jnp.log(jnp.broadcast_to(jnp.arange(1, D_STATE + 1, dtype=jnp.float32), (D_INNER, D_STATE))), 'D': jnp.ones((D_INNER,), dtype=jnp.float32), 'W_out': s(ks[7], (D_INNER, D_MODEL)), 'gn_gamma': jnp.ones((D_MODEL,), dtype=jnp.float32), 'gn_beta': jnp.zeros((D_MODEL,), dtype=jnp.float32)}
        return inp
    _L1_conv_all = _L1_conv_setup()
    _L1_conv_in = {k: v for k, v in _L1_conv_all.items() if k in ('W_in', 'conv_w', 'conv_b', 'W_x', 'W_dt', 'b_dt', 'A_log', 'D', 'W_out', 'gn_gamma', 'gn_beta', )}
    del _L1_conv_all

    return {
        "x": x,
        "L0_conv_od_weight": _L0_conv_in["od_weight"],
        "L0_conv_fc_w": _L0_conv_in["fc_w"],
        "L0_conv_bn_gamma": _L0_conv_in["bn_gamma"],
        "L0_conv_bn_beta": _L0_conv_in["bn_beta"],
        "L0_conv_bn_mean": _L0_conv_in["bn_mean"],
        "L0_conv_bn_var": _L0_conv_in["bn_var"],
        "L0_conv_ch_w": _L0_conv_in["ch_w"],
        "L0_conv_ch_b": _L0_conv_in["ch_b"],
        "L0_conv_sp_w": _L0_conv_in["sp_w"],
        "L0_conv_sp_b": _L0_conv_in["sp_b"],
        "L0_conv_ke_w": _L0_conv_in["ke_w"],
        "L0_conv_ke_b": _L0_conv_in["ke_b"],
        "L0_conv_b1_w": _L0_conv_in["b1_w"],
        "L0_conv_b1_b": _L0_conv_in["b1_b"],
        "L0_conv_b2_w": _L0_conv_in["b2_w"],
        "L0_conv_b2_b": _L0_conv_in["b2_b"],
        "L0_conv_ln_w": _L0_conv_in["ln_w"],
        "L0_conv_ln_b": _L0_conv_in["ln_b"],
        "L1_conv_W_in": _L1_conv_in["W_in"],
        "L1_conv_conv_w": _L1_conv_in["conv_w"],
        "L1_conv_conv_b": _L1_conv_in["conv_b"],
        "L1_conv_W_x": _L1_conv_in["W_x"],
        "L1_conv_W_dt": _L1_conv_in["W_dt"],
        "L1_conv_b_dt": _L1_conv_in["b_dt"],
        "L1_conv_A_log": _L1_conv_in["A_log"],
        "L1_conv_D": _L1_conv_in["D"],
        "L1_conv_W_out": _L1_conv_in["W_out"],
        "L1_conv_gn_gamma": _L1_conv_in["gn_gamma"],
        "L1_conv_gn_beta": _L1_conv_in["gn_beta"],
    }

def reference(x, L0_conv_od_weight, L0_conv_fc_w, L0_conv_bn_gamma, L0_conv_bn_beta, L0_conv_bn_mean, L0_conv_bn_var, L0_conv_ch_w, L0_conv_ch_b, L0_conv_sp_w, L0_conv_sp_b, L0_conv_ke_w, L0_conv_ke_b, L0_conv_b1_w, L0_conv_b1_b, L0_conv_b2_w, L0_conv_b2_b, L0_conv_ln_w, L0_conv_ln_b, L1_conv_W_in, L1_conv_conv_w, L1_conv_conv_b, L1_conv_W_x, L1_conv_W_dt, L1_conv_b_dt, L1_conv_A_log, L1_conv_D, L1_conv_W_out, L1_conv_gn_gamma, L1_conv_gn_beta):
    import jax
    import jax.numpy as jnp
    def _L0_conv_ref(x, od_weight, fc_w, bn_gamma, bn_beta, bn_mean, bn_var, ch_w, ch_b, sp_w, sp_b, ke_w, ke_b, b1_w, b1_b, b2_w, b2_b, ln_w, ln_b):
        import jax, jax.numpy as jnp
        import numpy as np
        BN_EPS = 1e-05
        LN_EPS = 1e-06
        B, C, H, W = x.shape
        K, _, _, KS, _ = od_weight.shape
        pooled = x.mean(axis=(2, 3))
        h = pooled @ fc_w.T
        h = (h - bn_mean) * (bn_gamma / jnp.sqrt(bn_var + BN_EPS)) + bn_beta
        h = jax.nn.relu(h)
        ch_att = jax.nn.sigmoid(h @ ch_w.T + ch_b)
        sp_att = jax.nn.sigmoid(h @ sp_w.T + sp_b).reshape(B, 1, 1, 1, KS, KS)
        ke_att = jax.nn.softmax(h @ ke_w.T + ke_b, axis=1).reshape(B, K, 1, 1, 1, 1)
        agg_w = jnp.sum(ke_att * sp_att * od_weight[None], axis=1)
        xs = x * ch_att[:, :, None, None]

        def dw(xb, wb):
            return jax.lax.conv_general_dilated(xb[None], wb, window_strides=(1, 1), padding=((1, 1), (1, 1)), feature_group_count=C)[0]
        y = jax.vmap(dw)(xs, agg_w)
        y1 = jnp.einsum('bchw,oc->bohw', y, b1_w) + b1_b[None, :, None, None]
        y2 = jnp.einsum('bchw,oc->bohw', y, b2_w) + b2_b[None, :, None, None]
        g = jax.nn.gelu(y1, approximate=False) * y2
        mu = g.mean(axis=1, keepdims=True)
        var = g.var(axis=1, keepdims=True)
        gn = (g - mu) / jnp.sqrt(var + LN_EPS)
        gn = gn * ln_w[None, :, None, None] + ln_b[None, :, None, None]
        return x + gn

    def _L1_conv_ref(x_hsi, W_in, conv_w, conv_b, W_x, W_dt, b_dt, A_log, D, W_out, gn_gamma, gn_beta):
        import jax, jax.numpy as jnp
        import numpy as np
        D_MODEL = 128
        D_STATE = 16
        D_CONV = 2
        EXPAND = 2
        D_INNER = EXPAND * D_MODEL
        DT_RANK = (D_MODEL + 15) // 16
        GROUPS = 4
        EPS = 1e-05

        def _causal_conv_k2(x, w, b):
            xp = jnp.pad(x, ((0, 0), (1, 0), (0, 0)))
            return xp[:, :-1] * w[:, 0] + xp[:, 1:] * w[:, 1] + b

        def _selective_scan(xc, dt, Bmat, Cmat, A, D):

            def step(h, inp):
                dt_t, B_t, C_t, x_t = inp
                dA = jnp.exp(dt_t[..., None] * A)
                dBx = dt_t[..., None] * B_t[:, None, :] * x_t[..., None]
                h = dA * h + dBx
                y = jnp.einsum('bdn,bn->bd', h, C_t)
                return (h, y)
            B_, L, Din = xc.shape
            h0 = jnp.zeros((B_, Din, A.shape[1]), dtype=xc.dtype)
            xs = (jnp.swapaxes(dt, 0, 1), jnp.swapaxes(Bmat, 0, 1), jnp.swapaxes(Cmat, 0, 1), jnp.swapaxes(xc, 0, 1))
            _, ys = jax.lax.scan(step, h0, xs)
            return jnp.swapaxes(ys, 0, 1) + xc * D

        def _mamba(x, W_in, conv_w, conv_b, W_x, W_dt, b_dt, A_log, D, W_out):
            xz = x @ W_in
            xh, z = jnp.split(xz, 2, axis=-1)
            xh = jax.nn.silu(_causal_conv_k2(xh, conv_w, conv_b))
            x_dbl = xh @ W_x
            dt_low = x_dbl[..., :DT_RANK]
            Bmat = x_dbl[..., DT_RANK:DT_RANK + D_STATE]
            Cmat = x_dbl[..., DT_RANK + D_STATE:]
            dt = jax.nn.softplus(dt_low @ W_dt + b_dt)
            A = -jnp.exp(A_log)
            y = _selective_scan(xh, dt, Bmat, Cmat, A, D)
            y = y * jax.nn.silu(z)
            return y @ W_out

        def _group_norm(x, gamma, beta):
            B_, C, H, W = x.shape
            xr = x.reshape(B_, GROUPS, -1)
            mean = xr.mean(-1, keepdims=True)
            var = xr.var(-1, keepdims=True)
            xn = ((xr - mean) * jax.lax.rsqrt(var + EPS)).reshape(B_, C, H, W)
            return xn * gamma[:, None, None] + beta[:, None, None]
        B_, C, H, W = x_hsi.shape
        x = jnp.transpose(x_hsi, (0, 2, 3, 1)).reshape(B_, H * W, C)
        x = _mamba(x, W_in, conv_w, conv_b, W_x, W_dt, b_dt, A_log, D, W_out)
        x = jnp.transpose(x.reshape(B_, H, W, C), (0, 3, 1, 2))
        x = jax.nn.silu(_group_norm(x, gn_gamma, gn_beta))
        return x + x_hsi

    def _gn(v, G=32, eps=1e-5):
        B_, C_, H_, W_ = v.shape
        g = v.reshape(B_, G, C_ // G, H_, W_)
        m = jnp.mean(g, axis=(2, 3, 4), keepdims=True)
        s = jnp.var(g, axis=(2, 3, 4), keepdims=True)
        return ((g - m) / jnp.sqrt(s + eps)).reshape(v.shape)

    def _ln_c(v, eps=1e-6):
        m = jnp.mean(v, axis=1, keepdims=True)
        s = jnp.var(v, axis=1, keepdims=True)
        return (v - m) / jnp.sqrt(s + eps)

    def _ln_t(v, eps=1e-5):
        m = jnp.mean(v, axis=-1, keepdims=True)
        s = jnp.var(v, axis=-1, keepdims=True)
        return (v - m) / jnp.sqrt(s + eps)

    def _to_tokens(v):
        B_, C_, H_, W_ = v.shape
        return v.reshape(B_, C_, H_ * W_).transpose(0, 2, 1)
    def _from_tokens(t, like):
        B_, C_, H_, W_ = like.shape
        return t.transpose(0, 2, 1).reshape(B_, C_, H_, W_)

    x = _L0_conv_ref(x, L0_conv_od_weight, L0_conv_fc_w, L0_conv_bn_gamma, L0_conv_bn_beta, L0_conv_bn_mean, L0_conv_bn_var, L0_conv_ch_w, L0_conv_ch_b, L0_conv_sp_w, L0_conv_sp_b, L0_conv_ke_w, L0_conv_ke_b, L0_conv_b1_w, L0_conv_b1_b, L0_conv_b2_w, L0_conv_b2_b, L0_conv_ln_w, L0_conv_ln_b)
    x = _L1_conv_ref(x, L1_conv_W_in, L1_conv_conv_w, L1_conv_conv_b, L1_conv_W_x, L1_conv_W_dt, L1_conv_b_dt, L1_conv_A_log, L1_conv_D, L1_conv_W_out, L1_conv_gn_gamma, L1_conv_gn_beta)
    return x


_drawn_inputs = setup_inputs


def setup_inputs(seed=0):
    import zlib

    import numpy as np

    out = dict(_drawn_inputs(seed))
    spreads = {'L0_conv_bn_gamma': (1.0, 0.6),
     'L0_conv_bn_beta': (0.0, 0.8),
     'L0_conv_bn_mean': (0.0, 0.8),
     'L0_conv_bn_var': (1.0, 0.6),
     'L0_conv_ch_b': (0.0, 0.681),
     'L0_conv_sp_b': (0.0, 0.576),
     'L0_conv_ke_b': (0.0, 0.293),
     'L0_conv_b1_b': (0.0, 0.1),
     'L0_conv_b2_b': (0.0, 0.1),
     'L0_conv_ln_w': (1.0, 0.2),
     'L0_conv_ln_b': (0.0, 0.1),
     'L1_conv_D': (1.0, 0.2),
     'L1_conv_gn_gamma': (1.0, 0.2),
     'L1_conv_gn_beta': (0.0, 0.1)}
    factors = {'L0_conv_fc_w': 8.0,
     'L0_conv_ch_w': 8.0,
     'L0_conv_sp_w': 8.0,
     'L0_conv_ke_w': 8.0,
     'L1_conv_W_x': 8.0,
     'L1_conv_W_dt': 8.0,
     'L1_conv_b_dt': 8.0,
     'L1_conv_A_log': 8.0}
    for name, (base, spread) in spreads.items():
        noise = np.random.default_rng([zlib.crc32(name.encode()), seed]).standard_normal(out[name].shape)
        drawn = base * np.exp(spread * noise) if base else spread * noise
        out[name] = jnp.asarray(drawn.astype(out[name].dtype))
    for name, factor in factors.items():
        out[name] = (out[name] * factor).astype(out[name].dtype)
    return out
```

```python
from contextlib import ExitStack

import concourse.bass as bass
import concourse.mybir as mybir
import numpy as np

F32 = mybir.dt.float32
BF16 = mybir.dt.bfloat16
ALU = mybir.AluOpType
ACT = mybir.ActivationFunctionType
AX = mybir.AxisListType

P = 128
H = W = 64
L = H * W
T = 512
CH = L // T
ROWS = T // W
DI = 2
NS = 16
DSUB = P // NS
SUB = 2 * P // DSUB
SLOTS = SUB // 2
QUADS = SUB // 4
R = 8
NDBL = R + 2 * NS
KK = 4
AA = 16
TAPS = 9
HQ = 3
RD = 4
RX = 3
BN_EPS, LN_EPS, GN_EPS = 1e-5, 1e-6, 1e-5
GROUPS = 4

PE_Y, PE_GC, PE_VAR, PE_XH, PE_DBL, PE_BC, PE_DT, PE_OUT, PE_Z = 0, 2, 3, (5, 6), 8, 9, 10, 11, 12
PE_CONV = {13: (0, 3), 14: (3, 6), 15: (6, 9)}
SUM_LAG = 5


def subgroup(i):
    u = i // 2
    return u // 8, 2 * (u % 2) + i % 2, (u % 8) // 2


def build_program(nc, a, out):
    B = a["x"].shape[0]
    x_d = a["x"].rearrange("b c h w -> b c (h w)")
    o_d = out.rearrange("b c h w -> b c (h w)")
    ctx = ExitStack()
    with ctx:
        def sb(name, shape, dt=F32):
            return ctx.enter_context(nc.sbuf_tensor(name, shape, dt))

        def sem(name):
            return ctx.enter_context(nc.semaphore(name))

        names = ["fc_wT", "bn", "ch_wT", "ch_b", "spke_wT", "spke_b", "od", "b1T", "b2T", "vec0", "W_in", "cw_rows",
                 "cb", "Wx", "wdt", "A_log", "Dv", "Wout", "gn", "ident", "center", "ones", "gblock", "bcsel", "selsum"]
        w = {n: sb("w_" + n, list(a[n].shape)) for n in names}
        selb = sb("selb", [96, 4, P], BF16)
        W_taps = sb("W_taps", [P, 2, 2 * P])
        A_neg = sb("A_neg", [P, SUB])
        wts = sb("wts", [P, B, TAPS])
        diag = sb("diag", [P, TAPS, P])
        eps = sb("eps", [P, 3])
        x1 = sb("x1", [P, 1 + L])
        o = sb("o", [P, L])
        osum = sb("osum", [P, 2, CH])
        gst = sb("gst", [P, 2])
        gmv = sb("gmv", [P, 6])
        xin = sb("xin", [P, 2, (ROWS + 2) * W])
        ysb = sb("ysb", [P, T])
        gbuf = sb("gbuf", [P, T])
        sq = sb("sq", [P, T])
        xh = sb("xh", [P, 2, DI, T])
        sz = sb("sz", [P, 2, DI, T])
        dbl = sb("dbl", [64, T])
        bc = sb("bc", [P, 2, 2, T])
        sp = sb("sp", [P, DI, T])
        dt = sb("dt", [P, DI, T])
        dtx = sb("dtx", [P, DI, T])
        res = sb("res", [P, DI, T])
        parts = {n: [sb(f"{n}_{k}", [P, DI, T], BF16) for k in ("hi", "mid", "lo")] for n in ("dt", "dtx")}
        stack = {n: sb(f"stack_{n}", [96, 2, DI * 4, T], BF16) for n in ("dt", "dtx")}
        dA = sb("dA", [P, RD, T])
        dbx = sb("dbx", [P, RD, T])
        hq = sb("hq", [P, HQ, 4, T])
        carry = sb("carry", [P, SUB])
        y = sb("y", [P, DI, T])
        ps_dt = ctx.enter_context(nc.psum_tensor("ps_dt", [P, 2, T], F32))
        ps_x = ctx.enter_context(nc.psum_tensor("ps_x", [P, RX, T], F32))
        ps_acc = ctx.enter_context(nc.psum_tensor("ps_acc", [P, T], F32))
        pp = ctx.enter_context(nc.psum_tensor("pp", [P, 2, T], F32))
        xp = o[:, :]
        pooled = gbuf[:, 0:B]
        hrep = x1[0:AA, 0:B * P].rearrange("p (b k) -> p b k", b=B)
        h_att = ysb[0:AA, 0:B]
        bn_s = ysb[0:AA, 64:68]
        spke = sq[:, 0:B * 13].rearrange("p (b k) -> p b k", b=B)
        ch_att = gbuf[:, 64:64 + B]
        kmx = gbuf[:, 128:128 + B]
        od_t = xh[:, 0, 0, 0:B * TAPS].rearrange("p (b k) -> p b k", b=B)

        (w_loaded, xpool_loaded, pool_done, setup_pe, setup_act, setup_dve, att_ready, consts_ready,
         batch_done, diag_ready, x_loaded_even, conv_done, y_evac, y12_done, gelu_done, g_done, gc_done, sq_done,
         var_done, rstd_done, x1_done, xh_mm, xh_done, dbl_mm, dbl_done, bc_mm, bc_done, dt_mm, sp_done, dt_done,
         dthi_done, dtres_done, dtmid_done, dtlo_done, dtx_done, dtxhi_done, dtxres_done, dtxmid_done, dtxlo_done,
         dt_stacked, dtx_stacked, z_mm, z_done, dtb_mm, exp_done, xb_mm, bmul_done, scan_done, cmul_done, carry_done,
         sum_done, yacc_done, yz_done, out_mm, o_done, gst_done, gmm_done, gmv_done, grs_done, gsc_done, silu_done,
         fin_done, stored, lnv_done, t_done, t2_done) = [sem(n) for n in (
             "w_loaded xpool_loaded pool_done setup_pe setup_act setup_dve att_ready consts_ready "
             "batch_done diag_ready x_loaded_even conv_done y_evac y12_done gelu_done g_done gc_done sq_done "
             "var_done rstd_done x1_done xh_mm xh_done dbl_mm dbl_done bc_mm bc_done dt_mm sp_done dt_done "
             "dthi_done dtres_done dtmid_done dtlo_done dtx_done dtxhi_done dtxres_done dtxmid_done dtxlo_done "
             "dt_stacked dtx_stacked z_mm z_done dtb_mm exp_done xb_mm bmul_done scan_done cmul_done carry_done "
             "sum_done yacc_done yz_done out_mm o_done gst_done gmm_done gmv_done grs_done gsc_done silu_done "
             "fin_done stored lnv_done t_done t2_done").split()]
        x_loaded = [x_loaded_even, sem("x_loaded_odd")]
        pair_seen = sem("pair_seen")
        stacked = {"dt": dt_stacked, "dtx": dtx_stacked}
        n_weights = len(names) + 1

        block = ctx.enter_context(nc.Block())
        mm = nc.tensor.matmul

        @block.sync
        def _(sp_e):
            for n in names:
                sp_e.dma_start(w[n][:], a[n]).then_inc(w_loaded, 16)
            sp_e.dma_start(dA[0:96, 0, :], a["selb"].rearrange("r e k -> r (e k)")).then_inc(w_loaded, 16)
            with sp_e.Fori(0, B, 1) as b:
                sp_e.wait_ge(pool_done, b + 1)
                sp_e.dma_start(xp, x_d[bass.ds(b, 1)].rearrange("o c l -> (o c) l")).then_inc(xpool_loaded, 16)

            def load_x(b, c):
                if c >= 2:
                    sp_e.wait_ge(x1_done, b * CH + c - 1)
                r0, r1 = max(ROWS * c - 1, 0), min(ROWS * (c + 1) + 1, H)
                d0 = r0 - (ROWS * c - 1)
                sp_e.dma_start(xin[:, c % 2, d0 * W:(d0 + r1 - r0) * W],
                               x_d[bass.ds(b, 1), :, r0 * W:r1 * W].rearrange("o c l -> (o c) l")).then_inc(x_loaded[c % 2], 16)

            def restack(b, c, n):
                done = {"dt": (dthi_done, dtmid_done, dtlo_done), "dtx": (dtxhi_done, dtxmid_done, dtxlo_done)}[n]
                for s in done:
                    sp_e.wait_ge(s, b * CH + c + 1)
                for k in range(3):
                    for j in range(4):
                        dst = stack[n][32 * k:32 * k + 32, c % 2, :, :].rearrange("p (d j) t -> p d j t", d=DI)[:, :, j, :]
                        sp_e.dma_start(dst, parts[n][k][32 * j:32 * j + 32, :, :]).then_inc(stacked[n], 16)

            with sp_e.Fori(0, B, 1) as b:
                sp_e.wait_ge(batch_done, b + 1)
                load_x(b, 0)
                load_x(b, 1)
                restack(b, 0, "dt")
                restack(b, 0, "dtx")
                for c in range(CH - 1):
                    if c + 2 < CH:
                        load_x(b, c + 2)
                    restack(b, c + 1, "dt")
                    restack(b, c + 1, "dtx")
                for k in range(4):
                    sp_e.wait_ge(fin_done, b * 4 + k + 1)
                    sp_e.dma_start(o_d[bass.ds(b, 1), :, k * (L // 4):(k + 1) * (L // 4)].rearrange("o c l -> (o c) l"),
                                   o[:, k * (L // 4):(k + 1) * (L // 4)]).then_inc(stored, 16)
            sp_e.wait_ge(stored, B * 64)

        @block.tensor
        def _(pe):
            pe.wait_ge(w_loaded, 16 * n_weights)
            pe.wait_ge(pool_done, B + 1)
            mm(pp[0:AA, 0, 0:B], w["fc_wT"][:], pooled, start=True, stop=True).then_inc(setup_pe, 1)
            pe.wait_ge(setup_dve, 3)
            mm(pp[:, 0, 0:B], w["ch_wT"][:], h_att, start=True, stop=True).then_inc(setup_pe, 1)
            for b in range(B):
                last = mm(pp[:, 1, 13 * b:13 * b + 13], hrep[:, b, :], w["spke_wT"][:], start=(b == 0), stop=True,
                          skip_group_check=True)
            last.then_inc(setup_pe, 1)

            def conv(b, c, t0, t1):
                taps = [4, 0, 1, 2, 3, 5, 6, 7, 8]
                rows = xin[:, c % 2, :].rearrange("p (r w) -> p r w", w=W)
                acc = pp[:, 0, :].rearrange("p (r w) -> p r w", w=W)
                for n in range(t0, t1):
                    kh, kw = divmod(taps[n], 3)
                    ra, rb = (1 if c == 0 and kh == 0 else 0), (ROWS - 1 if c == CH - 1 and kh == 2 else ROWS)
                    ca, cb = (1 if kw == 0 else 0), (W - 1 if kw == 2 else W)
                    last = mm(acc[:, ra:rb, ca:cb], diag[:, taps[n], :], rows[:, ra + kh:rb + kh, ca + kw - 1:cb + kw - 1],
                              start=(n == 0), stop=(n == TAPS - 1))
                if t1 == TAPS:
                    last.then_inc(conv_done, 1)

            def step_conv(b, c, t0, t1):
                if t0 == 0:
                    pe.wait_ge(x_loaded[c % 2], 16 * (b * (CH // 2) + c // 2 + 1))
                    if c:
                        pe.wait_ge(z_done, b * CH + c)
                conv(b, c, t0, t1)

            def step_y(b, c):
                pe.wait_ge(y_evac, b * CH + c + 1)
                mm(pp[:, 0, :], w["b1T"][:], ysb[:], start=True, stop=True)
                mm(pp[:, 1, :], w["b2T"][:], ysb[:], start=True, stop=True).then_inc(y12_done, 1)

            def step_gc(b, c):
                pe.wait_ge(g_done, b * CH + c + 1)
                mm(pp[:, 0, :], w["center"][:], gbuf[:], start=True, stop=True).then_inc(gc_done, 1)

            def step_var(b, c):
                pe.wait_ge(sq_done, b * CH + c + 1)
                mm(pp[:, 1, :], w["ones"][:], sq[:], start=True, stop=True).then_inc(var_done, 1)

            def step_xh(b, c, d):
                if d == 0:
                    pe.wait_ge(x1_done, b * CH + c + 1)
                mm(pp[:, d, :], W_taps[:, 1, d * P:(d + 1) * P], x1[:, 1 + c * T:1 + (c + 1) * T], start=True, stop=False)
                mm(pp[:, d, :], W_taps[:, 0, d * P:(d + 1) * P], x1[:, c * T:(c + 1) * T], start=False,
                   stop=True).then_inc(xh_mm, 1)

            def step_dbl(b, c):
                pe.wait_ge(xh_done, 2 * (b * CH + c + 1))
                for d in range(DI):
                    last = mm(pp[0:NDBL, 0, :], w["Wx"][:, d, :], xh[:, c % 2, d, :], start=(d == 0), stop=(d == 1))
                last.then_inc(dbl_mm, 1)

            def step_bc(b, c):
                pe.wait_ge(dbl_done, b * CH + c + 1)
                for k in range(2):
                    last = mm(pp[:, k, :], w["bcsel"][:, k, :], dbl[0:NDBL + 1, :], start=True, stop=True)
                last.then_inc(bc_mm, 1)

            def step_dt(b, c):
                pe.wait_ge(bc_done, b * CH + c + 1)
                for d in range(DI):
                    last = mm(pp[:, d, :], w["wdt"][:, d * P:(d + 1) * P], dbl[0:NDBL + 1, :], start=True, stop=True)
                last.then_inc(dt_mm, 1)

            def step_z(b, c):
                if c >= 2:
                    pe.wait_ge(o_done, b * CH + c - 1)
                else:
                    pe.wait_ge(dt_done, b * CH + c + 1)
                for d in range(DI):
                    last = mm(pp[:, d, :], w["W_in"][:, (2 + d) * P:(3 + d) * P], x1[:, 1 + c * T:1 + (c + 1) * T],
                              start=True, stop=True)
                last.then_inc(z_mm, 1)

            def step_out(b, c):
                pe.wait_ge(yz_done, b * CH + c + 1)
                if c + 2 < CH:
                    pe.wait_ge(dt_done, b * CH + c + 3)
                if c == CH - 1:
                    pe.wait_ge(o_done, b * CH + c)
                for d in range(DI):
                    last = mm(pp[:, 0, :], w["Wout"][:, d, :], y[:, d, :], start=(d == 0), stop=(d == 1))
                last.then_inc(out_mm, 1)

            def broadcast(b, c, u):
                for i in (2 * u, 2 * u + 1):
                    d, j, e = subgroup(i)
                    n = c * SUB + i
                    if i == 0:
                        pe.wait_ge(dt_stacked, 192 * (b * CH + c + 1))
                    if n >= 2:
                        pe.wait_ge(exp_done, b * CH * SUB + n - 1)
                    mm(ps_dt[:, i % 2, :], selb[:, e, :], stack["dt"][:, c % 2, 4 * d + j, :], start=True,
                       stop=True).then_inc(dtb_mm, 1)
                    if i == 0:
                        pe.wait_ge(dtx_stacked, 192 * (b * CH + c + 1))
                    if n >= RX:
                        pe.wait_ge(bmul_done, b * CH * SUB + n - RX + 1)
                    mm(ps_x[:, n % RX, :], selb[:, e, :], stack["dtx"][:, c % 2, 4 * d + j, :], start=True,
                       stop=True).then_inc(xb_mm, 1)

            def sum_states(b, c, m):
                q = c * QUADS + m
                pe.wait_ge(cmul_done, b * CH * SLOTS + 2 * q + 2)
                if m % 4 == 0 and q:
                    pe.wait_ge(yacc_done, b * CH * DI + q // 4)
                for k in range(4):
                    last = mm(ps_acc[32 * k:32 * k + 32, :], w["selsum"][:, m % 4, :], hq[:, q % HQ, k, :],
                              start=(m % 4 == 0), stop=(m % 4 == 3))
                last.then_inc(sum_done, 1)

            with pe.Fori(0, B, 1) as b:
                pe.wait_ge(diag_ready, b + 1)
                step_conv(b, 0, 0, TAPS)
                step_y(b, 0)
                step_gc(b, 0)
                step_var(b, 0)
                step_xh(b, 0, 0)
                step_xh(b, 0, 1)
                step_dbl(b, 0)
                step_bc(b, 0)
                step_dt(b, 0)
                step_z(b, 0)
                step_conv(b, 1, 0, TAPS)
                for c in range(CH):
                    for u in range(SLOTS):
                        broadcast(b, c, u)
                        if u % 2 == SUM_LAG % 2:
                            m = c * QUADS + (u - SUM_LAG) // 2
                            if m >= 0:
                                sum_states(b, m // QUADS, m % QUADS)
                        if c >= 1 and u == PE_OUT:
                            step_out(b, c - 1)
                        if c + 1 < CH:
                            if u == PE_Y:
                                step_y(b, c + 1)
                            if u == PE_GC:
                                step_gc(b, c + 1)
                            if u == PE_VAR:
                                step_var(b, c + 1)
                            if u in PE_XH:
                                step_xh(b, c + 1, PE_XH.index(u))
                            if u == PE_DBL:
                                step_dbl(b, c + 1)
                            if u == PE_BC:
                                step_bc(b, c + 1)
                            if u == PE_DT:
                                step_dt(b, c + 1)
                            if u == PE_Z:
                                step_z(b, c + 1)
                        if c + 2 < CH and u in PE_CONV:
                            step_conv(b, c + 2, *PE_CONV[u])
                sum_states(b, CH - 1, QUADS - 2)
                sum_states(b, CH - 1, QUADS - 1)
                step_out(b, CH - 1)
                pe.wait_ge(gst_done, b + 1)
                mm(pp[:, 1, 0:2], w["gblock"][:], gst[:], start=True, stop=True).then_inc(gmm_done, 1)

        @block.scalar
        def _(act):
            A = nc.scalar.activation
            act.wait_ge(w_loaded, 16 * n_weights)
            act.wait_ge(consts_ready, 4)
            with act.Fori(0, B, 1) as b:
                act.wait_ge(xpool_loaded, 16 * b + 16)
                A(xp, xp, ACT.Identity, scale=1.0 / L, accum_out=pooled[:, bass.ds(b, 1)]).then_inc(pool_done, 1)
            A(bn_s[:, 0:1], w["bn"][:, 3:4], ACT.Ln, bias=eps[0:AA, 0:1]).then_inc(setup_act, 1)
            act.wait_ge(setup_act, 1)
            A(bn_s[:, 1:2], bn_s[:, 0:1], ACT.Exp, scale=-0.5).then_inc(setup_act, 1)
            A(A_neg[:], w["A_log"][:], ACT.Exp).then_inc(setup_act, 1)
            act.wait_ge(setup_dve, 4)
            A(spke[:, :, 9:13], spke[:, :, 9:13], ACT.Exp).then_inc(setup_act, 1)
            act.wait_ge(setup_pe, 3)
            A(ch_att, pp[:, 0, 0:B], ACT.Sigmoid, bias=w["ch_b"][:]).then_inc(setup_act, 1)
            A(spke[:, :, 0:9], spke[:, :, 0:9], ACT.Sigmoid).then_inc(setup_act, 1)

            def evac_conv(b, c):
                act.wait_ge(conv_done, b * CH + c + 1)
                A(ysb[:], pp[:, 0, :], ACT.Copy).then_inc(y_evac, 1)

            def gelu(b, c):
                act.wait_ge(y12_done, b * CH + c + 1)
                A(gbuf[:], pp[:, 0, :], ACT.Gelu, bias=w["vec0"][:, 0:1]).then_inc(gelu_done, 1)

            def square(b, c):
                act.wait_ge(gc_done, b * CH + c + 1)
                A(sq[:], pp[:, 0, :], ACT.Square).then_inc(sq_done, 1)

            def rstd(b, c):
                act.wait_ge(var_done, b * CH + c + 1)
                A(sq[:], pp[:, 1, :], ACT.Ln, bias=eps[:, 1:2]).then_inc(lnv_done, 1)
                act.wait_ge(lnv_done, b * CH + c + 1)
                A(sq[:], sq[:], ACT.Exp, scale=-0.5).then_inc(rstd_done, 1)

            def silu_xh(b, c, d):
                act.wait_ge(xh_mm, 2 * (b * CH + c) + d + 1)
                if c >= 2 and d == 0:
                    act.wait_ge(yz_done, b * CH + c - 1)
                A(xh[:, c % 2, d, :], pp[:, d, :], ACT.Silu, bias=w["cb"][:, d:d + 1]).then_inc(xh_done, 1)

            def evac_dbl(b, c):
                act.wait_ge(dbl_mm, b * CH + c + 1)
                A(dbl[0:NDBL, :], pp[0:NDBL, 0, :], ACT.Copy).then_inc(dbl_done, 1)

            def evac_bc(b, c):
                act.wait_ge(bc_mm, b * CH + c + 1)
                if c >= 2:
                    act.wait_ge(cmul_done, (b * CH + c - 1) * SLOTS)
                A(bc[:, c % 2, :, :], pp[:, :, :], ACT.Copy).then_inc(bc_done, 1)

            def softplus_tail(b, c):
                act.wait_ge(dt_mm, b * CH + c + 1)
                A(sp[:], pp[:, :, :], ACT.Abs).then_inc(sp_done, 1)
                act.wait_ge(sp_done, 3 * (b * CH + c) + 1)
                A(sp[:], sp[:], ACT.Exp, scale=-1.0).then_inc(sp_done, 1)
                act.wait_ge(sp_done, 3 * (b * CH + c) + 2)
                A(sp[:], sp[:], ACT.Ln, bias=1.0).then_inc(sp_done, 1)

            def cast_part(b, c, n, k):
                src, ready, done = {("dt", 0): (dt, dt_done, dthi_done), ("dt", 1): (res, dtres_done, dtmid_done),
                                    ("dtx", 0): (dtx, dtx_done, dtxhi_done), ("dtx", 1): (res, dtxres_done, dtxmid_done)}[n, k]
                act.wait_ge(ready, b * CH + c + 1)
                if k == 0 and c:
                    act.wait_ge(stacked[n], 192 * (b * CH + c))
                A(parts[n][k][:], src[:], ACT.Copy).then_inc(done, 1)

            def silu_z(b, c):
                act.wait_ge(z_mm, b * CH + c + 1)
                if c >= 2:
                    act.wait_ge(yz_done, b * CH + c - 1)
                A(sz[:, c % 2, :, :], pp[:, :, :], ACT.Silu).then_inc(z_done, 1)

            def evac_out(b, c):
                act.wait_ge(out_mm, b * CH + c + 1)
                A(o[:, c * T:(c + 1) * T], pp[:, 0, :], ACT.Identity, accum_out=osum[:, 0, c:c + 1])
                A(y[:, 0, :], pp[:, 0, :], ACT.Square, accum_out=osum[:, 1, c:c + 1]).then_inc(o_done, 1)

            def decay(b, c, u):
                for i in (2 * u, 2 * u + 1):
                    n = c * SUB + i
                    act.wait_ge(dtb_mm, b * CH * SUB + n + 1)
                    if n >= RD:
                        act.wait_ge(scan_done, b * CH * SUB + n - RD + 1)
                    A(dA[:, i % RD, :], ps_dt[:, i % 2, :], ACT.Exp, scale=A_neg[:, i:i + 1]).then_inc(exp_done, 1)

            with act.Fori(0, B, 1) as b:
                act.wait_ge(batch_done, b + 1)
                evac_conv(b, 0)
                gelu(b, 0)
                square(b, 0)
                rstd(b, 0)
                silu_xh(b, 0, 0)
                silu_xh(b, 0, 1)
                evac_dbl(b, 0)
                evac_bc(b, 0)
                softplus_tail(b, 0)
                cast_part(b, 0, "dt", 0)
                cast_part(b, 0, "dt", 1)
                cast_part(b, 0, "dtx", 0)
                cast_part(b, 0, "dtx", 1)
                silu_z(b, 0)
                evac_conv(b, 1)
                for c in range(CH):
                    for u in range(SLOTS):
                        decay(b, c, u)
                        if c >= 1 and u == PE_OUT:
                            evac_out(b, c - 1)
                        if c + 1 < CH:
                            if u == PE_Y:
                                gelu(b, c + 1)
                            if u == PE_GC:
                                square(b, c + 1)
                            if u == PE_VAR:
                                rstd(b, c + 1)
                            if u in PE_XH:
                                silu_xh(b, c + 1, PE_XH.index(u))
                            if u == PE_DBL:
                                evac_dbl(b, c + 1)
                            if u == PE_BC:
                                evac_bc(b, c + 1)
                            if u == PE_DT:
                                softplus_tail(b, c + 1)
                            if u == PE_DT + 1:
                                cast_part(b, c + 1, "dt", 0)
                            if u == PE_Z:
                                silu_z(b, c + 1)
                                cast_part(b, c + 1, "dtx", 0)
                            if u == PE_Z + 1:
                                cast_part(b, c + 1, "dt", 1)
                            if u == PE_Z + 2:
                                cast_part(b, c + 1, "dtx", 1)
                        if c + 2 < CH and u == 15:
                            evac_conv(b, c + 2)
                evac_out(b, CH - 1)
                act.wait_ge(gmv_done, 3 * b + 3)
                A(gmv[:, 2:3], gmv[:, 2:3], ACT.Ln, bias=eps[:, 2:3]).then_inc(grs_done, 1)
                act.wait_ge(grs_done, 2 * b + 1)
                A(gmv[:, 3:4], gmv[:, 2:3], ACT.Exp, scale=-0.5).then_inc(grs_done, 1)
                act.wait_ge(gsc_done, 3 * b + 3)
                for k in range(4):
                    piece = o[:, k * (L // 4):(k + 1) * (L // 4)]
                    A(piece, piece, ACT.Silu, scale=gmv[:, 4:5], bias=gmv[:, 5:6]).then_inc(silu_done, 1)

        @block.vector
        def _(dve):
            v = nc.vector
            for k, e in enumerate((BN_EPS, LN_EPS, GN_EPS)):
                v.memset(eps[:, k:k + 1], e).then_inc(consts_ready, 1)
            v.memset(dbl[:], 1.0).then_inc(consts_ready, 1)
            v.memset(bn_s[:, 2:3], 0.0).then_inc(pool_done, 1)
            dve.wait_ge(w_loaded, 16 * n_weights)
            v.tensor_copy(selb[:].rearrange("r e k -> r (e k)"), dA[0:96, 0, :])
            dve.wait_ge(setup_act, 2)
            dve.wait_ge(setup_pe, 1)
            v.tensor_tensor(bn_s[:, 2:3], bn_s[:, 1:2], w["bn"][:, 0:1], ALU.mult).then_inc(setup_dve, 1)
            dve.wait_ge(setup_dve, 1)
            v.tensor_scalar(h_att, pp[0:AA, 0, 0:B], w["bn"][:, 2:3], bn_s[:, 2:3], ALU.subtract, ALU.mult).then_inc(setup_dve, 1)
            dve.wait_ge(setup_dve, 2)
            v.tensor_scalar(h_att, h_att, w["bn"][:, 1:2], 0.0, ALU.add, ALU.max).then_inc(t_done, 1)
            dve.wait_ge(t_done, 1)
            v.tensor_copy(hrep, h_att.unsqueeze(2).to_broadcast([AA, B, P])).then_inc(setup_dve, 1)
            dve.wait_ge(setup_pe, 3)
            v.tensor_tensor(spke, pp[:, 1, 0:13 * B].rearrange("p (b k) -> p b k", b=B),
                            w["spke_b"][:].unsqueeze(1).to_broadcast([P, B, 13]), ALU.add).then_inc(t_done, 1)
            dve.wait_ge(t_done, 2)
            v.tensor_reduce(kmx.unsqueeze(2), spke[:, :, 9:13], AX.X, ALU.max).then_inc(t_done, 1)
            dve.wait_ge(t_done, 3)
            v.tensor_tensor(spke[:, :, 9:13], spke[:, :, 9:13], kmx.unsqueeze(2).to_broadcast([P, B, KK]),
                            ALU.subtract).then_inc(setup_dve, 1)
            dve.wait_ge(setup_act, 6)
            v.tensor_reduce(kmx.unsqueeze(2), spke[:, :, 9:13], AX.X, ALU.add).then_inc(t_done, 1)
            dve.wait_ge(t_done, 4)
            v.reciprocal(kmx, kmx).then_inc(t_done, 1)
            dve.wait_ge(t_done, 5)
            v.tensor_tensor(kmx, kmx, ch_att, ALU.mult).then_inc(t_done, 1)
            n = 6
            for k in range(KK):
                dst = wts[:] if k == 0 else od_t
                dve.wait_ge(t_done, n)
                v.tensor_tensor(dst, w["od"][:, k, :].unsqueeze(1).to_broadcast([P, B, TAPS]),
                                spke[:, :, 9 + k:10 + k].to_broadcast([P, B, TAPS]), ALU.mult).then_inc(t_done, 1)
                n += 1
                if k:
                    dve.wait_ge(t_done, n)
                    v.tensor_tensor(wts[:], wts[:], od_t, ALU.add).then_inc(t_done, 1)
                    n += 1
            dve.wait_ge(t_done, n)
            v.tensor_tensor(wts[:], wts[:], spke[:, :, 0:9], ALU.mult).then_inc(t_done, 1)
            dve.wait_ge(t_done, n + 1)
            v.tensor_tensor(wts[:], wts[:], kmx.unsqueeze(2).to_broadcast([P, B, TAPS]), ALU.mult).then_inc(t_done, 1)
            setup_t = n + 2
            v.tensor_scalar(A_neg[:], A_neg[:], -1.0, None, ALU.mult)
            for k in range(2):
                v.tensor_tensor(W_taps[:, k, :], w["W_in"][:, 0:2 * P], w["cw_rows"][:, k, :], ALU.mult)
            v.memset(x1[:, 0:1], 0.0).then_inc(batch_done, 1)
            dve.wait_ge(t_done, setup_t)
            dve.wait_ge(batch_done, 1)

            def gate(b, c):
                dve.wait_ge(gelu_done, b * CH + c + 1)
                v.scalar_tensor_tensor(gbuf[:], pp[:, 1, :], w["vec0"][:, 1:2], gbuf[:], ALU.add, ALU.mult).then_inc(g_done, 1)

            def norm_residual(b, c):
                dve.wait_ge(rstd_done, b * CH + c + 1)
                v.scalar_tensor_tensor(gbuf[:], pp[:, 0, :], w["vec0"][:, 2:3], sq[:], ALU.mult, ALU.mult).then_inc(t2_done, 1)
                dve.wait_ge(t2_done, b * CH + c + 1)
                v.scalar_tensor_tensor(x1[:, 1 + c * T:1 + (c + 1) * T], gbuf[:], w["vec0"][:, 3:4],
                                       xin[:, c % 2, W:W + T], ALU.add, ALU.add).then_inc(x1_done, 1)

            def softplus(b, c):
                dve.wait_ge(sp_done, 3 * (b * CH + c + 1))
                if c:
                    dve.wait_ge(dtx_done, b * CH + c)
                v.scalar_tensor_tensor(dt[:], pp[:, :, :], 0.0, sp[:], ALU.max, ALU.add).then_inc(dt_done, 1)

            def dt_rest(b, c):
                dve.wait_ge(dthi_done, b * CH + c + 1)
                if c:
                    dve.wait_ge(dtxlo_done, b * CH + c)
                v.tensor_tensor(res[:], dt[:], parts["dt"][0][:], ALU.subtract).then_inc(dtres_done, 1)

            def dtx_low(b, c):
                dve.wait_ge(dtxmid_done, b * CH + c + 1)
                v.tensor_tensor(parts["dtx"][2][:], res[:], parts["dtx"][1][:], ALU.subtract).then_inc(dtxlo_done, 1)

            def y_acc(b, c, d):
                dve.wait_ge(sum_done, b * CH * QUADS + c * QUADS + 4 * (d + 1))
                if d == 0 and c:
                    dve.wait_ge(o_done, b * CH + c)
                v.scalar_tensor_tensor(y[:, d, :], xh[:, c % 2, d, :], w["Dv"][:, d:d + 1], ps_acc[:], ALU.mult,
                                       ALU.add).then_inc(yacc_done, 1)

            def y_gate(b, c):
                dve.wait_ge(yacc_done, 2 * (b * CH + c + 1))
                dve.wait_ge(z_done, b * CH + c + 1)
                v.tensor_tensor(y[:], y[:], sz[:, c % 2, :, :], ALU.mult).then_inc(yz_done, 1)

            def scan_slot(b, c, u):
                for i in (2 * u, 2 * u + 1):
                    n = c * SUB + i
                    if i == 0:
                        dve.wait_ge(bc_done, b * CH + c + 1)
                    dve.wait_ge(xb_mm, b * CH * SUB + n + 1)
                    if n >= RD:
                        dve.wait_ge(scan_done, b * CH * SUB + n - RD + 1)
                    v.tensor_tensor(dbx[:, i % RD, :], ps_x[:, n % RX, :], bc[:, c % 2, 0, :], ALU.mult).then_inc(bmul_done, 1)
                for i in (2 * u, 2 * u + 1):
                    n = c * SUB + i
                    q = n // 4
                    dve.wait_ge(bmul_done, b * CH * SUB + n + 1)
                    dve.wait_ge(exp_done, b * CH * SUB + n + 1)
                    if q >= HQ:
                        dve.wait_ge(sum_done, b * CH * QUADS + q - HQ + 1)
                    if c:
                        dve.wait_ge(carry_done, b * CH * SLOTS + (c - 1) * SLOTS + u + 1)
                    v.tensor_tensor_scan(hq[:, q % HQ, i % 4, :], dA[:, i % RD, :], dbx[:, i % RD, :],
                                         carry[:, i:i + 1] if c else 0.0, ALU.mult, ALU.add).then_inc(scan_done, 1)

            with dve.Fori(0, B, 1) as b:
                v.tensor_tensor(diag[:], w["ident"][:].unsqueeze(1).to_broadcast([P, TAPS, P]),
                                wts[:, bass.ds(b, 1), :].rearrange("p o k -> p (o k)").unsqueeze(2).to_broadcast([P, TAPS, P]),
                                ALU.mult).then_inc(diag_ready, 1)
                gate(b, 0)
                norm_residual(b, 0)
                softplus(b, 0)
                dt_rest(b, 0)
                dtx_low(b, 0)
                for c in range(CH):
                    for u in range(SLOTS):
                        scan_slot(b, c, u)
                        if c >= 1 and u == 4:
                            y_acc(b, c - 1, 1)
                            y_gate(b, c - 1)
                        if u == 12:
                            y_acc(b, c, 0)
                        if c + 1 < CH:
                            if u == 1:
                                gate(b, c + 1)
                            if u == 4:
                                norm_residual(b, c + 1)
                            if u == PE_DT + 1:
                                softplus(b, c + 1)
                            if u == PE_DT + 2:
                                dt_rest(b, c + 1)
                            if u == 15:
                                dtx_low(b, c + 1)
                y_acc(b, CH - 1, 1)
                y_gate(b, CH - 1)
                dve.wait_ge(o_done, b * CH + CH)
                v.tensor_reduce(gst[:].unsqueeze(2), osum[:], AX.X, ALU.add).then_inc(gst_done, 1)
                dve.wait_ge(gmm_done, b + 1)
                v.tensor_copy(gmv[:, 0:2], pp[:, 1, 0:2]).then_inc(gmv_done, 1)
                dve.wait_ge(gmv_done, 3 * b + 1)
                v.scalar_tensor_tensor(gmv[:, 2:3], gmv[:, 0:1], gmv[:, 0:1], gmv[:, 1:2], ALU.mult,
                                       ALU.subtract).then_inc(gmv_done, 1)
                dve.wait_ge(gmv_done, 3 * b + 2)
                v.tensor_scalar(gmv[:, 2:3], gmv[:, 2:3], -1.0, 0.0, ALU.mult, ALU.max).then_inc(gmv_done, 1)
                dve.wait_ge(grs_done, 2 * b + 2)
                v.tensor_tensor(gmv[:, 4:5], gmv[:, 3:4], w["gn"][:, 0:1], ALU.mult).then_inc(gsc_done, 1)
                dve.wait_ge(gsc_done, 3 * b + 1)
                v.tensor_tensor(gmv[:, 5:6], gmv[:, 0:1], gmv[:, 4:5], ALU.mult).then_inc(gsc_done, 1)
                dve.wait_ge(gsc_done, 3 * b + 2)
                v.tensor_tensor(gmv[:, 5:6], w["gn"][:, 1:2], gmv[:, 5:6], ALU.subtract).then_inc(gsc_done, 1)
                for k in range(4):
                    s = slice(k * (L // 4), (k + 1) * (L // 4))
                    dve.wait_ge(silu_done, 4 * b + k + 1)
                    ins = v.tensor_tensor(o[:, s], o[:, s], x1[:, 1 + s.start:1 + s.stop], ALU.add)
                    ins.then_inc(fin_done, 1)
                dve.wait_ge(fin_done, 4 * b + 4)
                dve.wait_ge(stored, 64 * b + 64)
                v.memset(gst[:, 0:1], 0.0).then_inc(batch_done, 1)

        @block.gpsimd
        def _(pool):
            g = nc.gpsimd

            def dt_low(b, c):
                pool.wait_ge(dtmid_done, b * CH + c + 1)
                g.tensor_tensor(parts["dt"][2][:], res[:], parts["dt"][1][:], ALU.subtract).then_inc(dtlo_done, 1)

            def dt_x(b, c):
                pool.wait_ge(dt_done, b * CH + c + 1)
                g.tensor_tensor(dtx[:], dt[:], xh[:, c % 2, :, :], ALU.mult).then_inc(dtx_done, 1)

            def dtx_rest(b, c):
                pool.wait_ge(dtxhi_done, b * CH + c + 1)
                pool.wait_ge(dtlo_done, b * CH + c + 1)
                g.tensor_tensor(res[:], dtx[:], parts["dtx"][0][:], ALU.subtract).then_inc(dtxres_done, 1)

            def weigh_states(b, c, u):
                n = c * SLOTS + u
                pair = hq[:, (n // 2) % HQ, 2 * (n % 2):2 * (n % 2) + 2, :]
                pool.wait_ge(scan_done, b * CH * SUB + 2 * n + 2)
                pool.sem_inc(pair_seen, 1)
                g.tensor_copy(carry[:, 2 * u:2 * u + 2].unsqueeze(2), pair[:, :, T - 1:T]).then_inc(carry_done, 1)
                pool.wait_ge(carry_done, b * CH * SLOTS + n + 1)
                g.tensor_tensor(pair, pair, bc[:, c % 2, 1, :].unsqueeze(1).to_broadcast([P, 2, T]),
                                ALU.mult).then_inc(cmul_done, 1)

            with pool.Fori(0, B, 1) as b:
                pool.wait_ge(batch_done, b + 1)
                dt_x(b, 0)
                dt_low(b, 0)
                dtx_rest(b, 0)
                for c in range(CH):
                    for u in range(SLOTS):
                        weigh_states(b, c, u)
                        if c + 1 < CH:
                            if u == PE_DT + 1:
                                dt_x(b, c + 1)
                            if u == PE_DT + 3:
                                dt_low(b, c + 1)
                                dtx_rest(b, c + 1)


def _layout(i):
    f = lambda n: np.asarray(i[n])
    c = np.ascontiguousarray
    a = {"x": f("x")}
    a["fc_wT"] = f("L0_conv_fc_w").T
    a["bn"] = np.stack([f("L0_conv_bn_gamma"), f("L0_conv_bn_beta"), f("L0_conv_bn_mean"), f("L0_conv_bn_var")], 1)
    a["ch_wT"] = f("L0_conv_ch_w").T
    a["ch_b"] = f("L0_conv_ch_b")[:, None]
    a["spke_wT"] = np.concatenate([f("L0_conv_sp_w"), f("L0_conv_ke_w")], 0).T
    a["spke_b"] = np.repeat(np.concatenate([f("L0_conv_sp_b"), f("L0_conv_ke_b")])[None], P, 0)
    a["od"] = f("L0_conv_od_weight").reshape(KK, P, TAPS).transpose(1, 0, 2)
    a["b1T"] = f("L0_conv_b1_w").T
    a["b2T"] = f("L0_conv_b2_w").T
    a["vec0"] = np.stack([f("L0_conv_b1_b"), f("L0_conv_b2_b"), f("L0_conv_ln_w"), f("L0_conv_ln_b")], 1)
    a["W_in"] = f("L1_conv_W_in")
    a["cw_rows"] = np.repeat(f("L1_conv_conv_w").T[None], P, 0)
    a["cb"] = f("L1_conv_conv_b").reshape(DI, P).T
    a["Wx"] = f("L1_conv_W_x").reshape(DI, P, NDBL).transpose(1, 0, 2)
    wdt = np.zeros((NDBL + 1, 2 * P), np.float32)
    wdt[0:R] = f("L1_conv_W_dt")
    wdt[NDBL] = f("L1_conv_b_dt")
    a["wdt"] = wdt
    al = f("L1_conv_A_log").reshape(DI, 4, 4, P)
    a["A_log"] = np.stack([al[d, j, e] for d, j, e in map(subgroup, range(SUB))], 1)
    a["Dv"] = f("L1_conv_D").reshape(DI, P).T
    a["Wout"] = f("L1_conv_W_out").reshape(DI, P, P).transpose(1, 0, 2)
    a["gn"] = np.stack([f("L1_conv_gn_gamma"), f("L1_conv_gn_beta")], 1)
    a["ident"] = np.eye(P, dtype=np.float32)
    a["center"] = np.eye(P, dtype=np.float32) - np.float32(1 / P)
    a["ones"] = np.full((P, P), 1 / P, np.float32)
    a["gblock"] = np.kron(np.eye(GROUPS), np.full((P // GROUPS,) * 2, GROUPS / P / L)).astype(np.float32)
    part = np.arange(P)
    bcsel = np.zeros((NDBL + 1, 2, P), np.float32)
    for k in range(2):
        bcsel[R + NS * k + part % NS, k, part] = 1
    a["bcsel"] = bcsel
    selsum = np.zeros((P, 4, 32), np.float32)
    selb = np.zeros((96, 4, P), np.float32)
    for e in range(4):
        selsum[part, e, DSUB * e + part // NS] = 1
        for k in range(3):
            selb[32 * k + DSUB * e + part // NS, e, part] = 1
    a["selsum"], a["selb"] = selsum, selb
    return {k: c(v) for k, v in a.items()}


def kernel(**inputs):
    import concourse.bacc as _bacc
    from concourse.bass_utils import run_bass_kernel_spmd as _run

    arrays = _layout(inputs)
    nc = _bacc.Bacc("TRN2", target_bir_lowering=False, num_devices=1)
    args = {n: nc.dram_tensor(f"in_{n}", v.shape, mybir.dt.from_np(v.dtype), kind="ExternalInput").ap()
            for n, v in arrays.items()}
    out = nc.dram_tensor("out", arrays["x"].shape, F32, kind="ExternalOutput").ap()
    build_program(nc, args, out)
    r = _run(nc, [{f"in_{n}": v for n, v in arrays.items()}], core_ids=[0])
    return r.results[0]["out"]
```

```python
from contextlib import ExitStack

import concourse.bass as bass
import concourse.mybir as mybir
import numpy as np

F32 = mybir.dt.float32
BF16 = mybir.dt.bfloat16
ALU = mybir.AluOpType
ACT = mybir.ActivationFunctionType
AX = mybir.AxisListType
LN_EXP = "natural_log_exp_and_others"

P = 128
H = W = 64
L = H * W
T = 512
CH = L // T
ROWS = T // W
DI = 2
NS = 16
DSUB = P // NS
SUB = 2 * P // DSUB
SLOTS = SUB // 2
QUADS = SUB // 4
R = 8
NDBL = R + 2 * NS
KK = 4
AA = 16
TAPS = 9
HQ = 4
RD = 4
RX = 3
BN_EPS, LN_EPS, GN_EPS = 1e-5, 1e-6, 1e-5
GROUPS = 4

PE_XH, PE_DBL, PE_BC, PE_DT, PE_Z = (3, 5), 7, 11, 13, 17
ACT_XH, ACT_DBL, ACT_BC, ACT_SP, ACT_Z = 5, 10, 11, (13, 13, 13), 17
ACT_DTHI, ACT_DTMID, ACT_DTXHI, ACT_DTXMID = 16, 18, 20, 25
DVE_NORM, DVE_DT, DVE_DTREST, DVE_DTXLOW = (0, 0), 14, 16, 26
POOL_DTX, POOL_DTLOW, POOL_DTXREST = 7, 8, 8
PE_CONV = (19, 19, 19, 21, 22, 22, 23, 25, 26)
PE_Y, PE_GC, PE_VAR = 28, 30, 31
ACT_CONV, ACT_GELU, ACT_SQ, ACT_RSTD = 26, 28, 31, 31
DVE_GATE = 27
PE_OUT, ACT_OUT, DVE_Y1, DVE_YZ = 17, 17, 6, 14
DVE_Y0 = 23
SUM_LAG = 11
GN_SUM = 10



def last_use(i):
    return RX if i >= RX else next(SUB + i - j for j in range(SUB - 1, 0, -1) if j % RX == i % RX)


def subgroup(i):
    u = i // 2
    return u // 8, 2 * (u % 2) + i % 2, (u % 8) // 2


def build_program(nc, a, out):
    B = a["x"].shape[0]
    x_d = a["x"].rearrange("b c h w -> b c (h w)")
    o_d = out.rearrange("b c h w -> b c (h w)")
    ctx = ExitStack()
    with ctx:
        def sb(name, shape, dt=F32):
            return ctx.enter_context(nc.sbuf_tensor(name, shape, dt))

        def sem(name):
            return ctx.enter_context(nc.semaphore(name))

        names = ["fc_wT", "bn", "ch_wT", "ch_b", "spke_wT", "spke_b", "od", "b1T", "b2T", "vec0", "W_in", "cw_rows",
                 "cb", "Wx", "wdt", "A_log", "Dv", "Wout", "gn", "ident", "center", "ones", "gblock", "bcsel", "selsum"]
        w = {n: sb("w_" + n, list(a[n].shape)) for n in names}
        selb = sb("selb", [96, 4, P], BF16)
        W_taps = sb("W_taps", [P, 2, 2 * P])
        A_neg = sb("A_neg", [P, SUB])
        wts = sb("wts", [P, B, TAPS])
        diag = sb("diag", [P, TAPS, P])
        eps = sb("eps", [P, 3])
        x1 = sb("x1", [P, 1 + L])
        x1n = sb("x1n", [P, 1 + 2 * T])
        o = sb("o", [P, L])
        osum = sb("osum", [P, 2, CH])
        gst = sb("gst", [P, 2])
        gmv = sb("gmv", [P, 6])
        xin = sb("xin", [P, 2, (ROWS + 2) * W])
        ysb = sb("ysb", [P, T])
        gbuf = sb("gbuf", [P, T])
        sq = sb("sq", [P, T])
        xh = sb("xh", [P, 4, DI, T])
        sz = sb("sz", [P, 2, DI, T])
        dbl = sb("dbl", [64, T])
        bc = sb("bc", [P, 2, 2, T])
        sp = sb("sp", [P, DI, T])
        dt = sb("dt", [P, DI, T])
        dtx = dt
        res = sp
        parts = {n: [sb(f"{n}_{k}", [P, DI, T], BF16) for k in ("hi", "mid", "lo")] for n in ("dt", "dtx")}
        stack = {n: sb(f"stack_{n}", [96, 2, DI * 4, T], BF16) for n in ("dt", "dtx")}
        dA = sb("dA", [P, RD, T])
        dbx = sb("dbx", [P, RD, T])
        hq = sb("hq", [P, HQ, 4, T])
        carry = sb("carry", [P, SUB])
        y = sb("y", [P, DI, T])
        ps_dt = ctx.enter_context(nc.psum_tensor("ps_dt", [P, 2, T], F32))
        ps_x = ctx.enter_context(nc.psum_tensor("ps_x", [P, RX, T], F32))
        ps_acc = ctx.enter_context(nc.psum_tensor("ps_acc", [P, T], F32))
        pp = ctx.enter_context(nc.psum_tensor("pp", [P, 2, T], F32))
        def x1_cols(c, shift=0):
            c = c % CH
            return (x1n if c < 2 else x1)[:, 1 - shift + c * T:1 - shift + (c + 1) * T]

        xp = (o[:, :], x1[:, 1:1 + L])
        pooled = gbuf[:, 0:B].rearrange("p (k h) -> p k h", k=2)
        hrep = x1[0:AA, 0:B * P].rearrange("p (b k) -> p b k", b=B)
        h_att = ysb[0:AA, 0:B]
        bn_s = ysb[0:AA, 64:68]
        spke = sq[:, 0:B * 13].rearrange("p (b k) -> p b k", b=B)
        ch_att = gbuf[:, 64:64 + B]
        kmx = gbuf[:, 128:128 + B]
        od_t = xh[:, 0, 0, 0:B * TAPS].rearrange("p (b k) -> p b k", b=B)

        (w_loaded, xpool_loaded_even, pool_done, setup_pe, setup_act, setup_dve, att_ready, consts_ready,
         batch_done, diag_ready, x_loaded_even, conv_done, y_evac, y12_done, gelu_done, g_done, gc_done, sq_done,
         var_done, rstd_done, x1_done, xh_mm, xh_done, dbl_mm, dbl_done, bc_mm, bc_done, dt_mm, sp_done, dt_done,
         dthi_done, dtres_done, dtmid_done, dtlo_done, dtx_done, dtxhi_done, dtxres_done, dtxmid_done, dtxlo_done,
         dt_stacked, dtx_stacked, z_mm, z_done, dtb_mm, exp_done, xb_mm, bmul_done, scan_done, cmul_done, carry_done,
         sum_done, yacc_done, yz_done, out_mm, o_done, gst_done, gmm_done, gmv_done, grs_done, gsc_done, silu_done,
         fin_done, stored, lnv_done, t_done, t2_done) = [sem(n) for n in (
             "w_loaded xpool_loaded_even pool_done setup_pe setup_act setup_dve att_ready consts_ready "
             "batch_done diag_ready x_loaded_even conv_done y_evac y12_done gelu_done g_done gc_done sq_done "
             "var_done rstd_done x1_done xh_mm xh_done dbl_mm dbl_done bc_mm bc_done dt_mm sp_done dt_done "
             "dthi_done dtres_done dtmid_done dtlo_done dtx_done dtxhi_done dtxres_done dtxmid_done dtxlo_done "
             "dt_stacked dtx_stacked z_mm z_done dtb_mm exp_done xb_mm bmul_done scan_done cmul_done carry_done "
             "sum_done yacc_done yz_done out_mm o_done gst_done gmm_done gmv_done grs_done gsc_done silu_done "
             "fin_done stored lnv_done t_done t2_done").split()]
        x_loaded = [x_loaded_even, sem("x_loaded_odd")]
        pair_seen, wait_taken = sem("pair_seen"), sem("wait_taken")
        xpool_loaded = [xpool_loaded_even, sem("xpool_loaded_odd")]
        stacked = {"dt": dt_stacked, "dtx": dtx_stacked}
        n_weights = len(names) + 1

        block = ctx.enter_context(nc.Block())
        mm = nc.tensor.matmul

        @block.sync
        def _(sp_e):
            for n in names:
                sp_e.dma_start(w[n][:], a[n]).then_inc(w_loaded, 16)
            sp_e.dma_start(dA[0:96, 0, :], a["selb"].rearrange("r e k -> r (e k)")).then_inc(w_loaded, 16)

            def load_image(b, k):
                sp_e.dma_start(xp[k], x_d[bass.ds(b, 1)].rearrange("o c l -> (o c) l")).then_inc(xpool_loaded[k], 16)

            load_image(0, 0)
            load_image(1, 1)
            with sp_e.Fori(1, B // 2, 1) as h:
                for k in range(2):
                    sp_e.wait_ge(pool_done, 2 * h + k - 1)
                    sp_e.sem_inc(wait_taken, 1)
                    load_image(2 * h + k, k)

            def load_x(b, c):
                if not (isinstance(b, int) and b * CH + c < 2):
                    sp_e.wait_ge(x1_done, b * CH + c - 1)
                    sp_e.sem_inc(wait_taken, 1)
                r0, r1 = max(ROWS * (c % CH) - 1, 0), min(ROWS * (c % CH + 1) + 1, H)
                d0 = r0 - (ROWS * (c % CH) - 1)
                sp_e.dma_start(xin[:, c % 2, d0 * W:(d0 + r1 - r0) * W],
                               x_d[bass.ds(b + c // CH, 1), :, r0 * W:r1 * W].rearrange("o c l -> (o c) l")
                               ).then_inc(x_loaded[c % 2], 16)

            def restack(b, c, n):
                done = {"dt": (dthi_done, dtmid_done, dtlo_done), "dtx": (dtxhi_done, dtxmid_done, dtxlo_done)}[n]
                for k in range(3):
                    sp_e.wait_ge(done[k], b * CH + c + 1)
                    for j in range(4):
                        dst = stack[n][32 * k:32 * k + 32, c % 2, :, :].rearrange("p (d j) t -> p d j t", d=DI)[:, :, j, :]
                        sp_e.dma_start(dst, parts[n][k][32 * j:32 * j + 32, :, :]).then_inc(stacked[n], 16)

            def store(b):
                for k in range(4):
                    sp_e.wait_ge(fin_done, b * 4 + k + 1)
                    sp_e.sem_inc(wait_taken, 1)
                    sp_e.dma_start(o_d[bass.ds(b, 1), :, k * (L // 4):(k + 1) * (L // 4)].rearrange("o c l -> (o c) l"),
                                   o[:, k * (L // 4):(k + 1) * (L // 4)]).then_inc(stored, 16)

            def chunk(b, c, end):
                if c + 2 < end:
                    load_x(b, c + 2)
                if c + 1 < end:
                    restack(b, c + 1, "dt")
                    restack(b, c + 1, "dtx")
                if c == CH:
                    store(b)

            sp_e.wait_ge(batch_done, 1)
            load_x(0, 0)
            load_x(0, 1)
            restack(0, 0, "dt")
            restack(0, 0, "dtx")
            chunk(0, 0, CH + 3)
            with sp_e.Fori(0, B - 1, 1) as b:
                for c in range(1, CH + 1):
                    chunk(b, c, CH + 3)
            for c in range(1, CH):
                chunk(B - 1, c, CH)
            store(B - 1)
            sp_e.wait_ge(stored, B * 64 + 16)

        @block.tensor
        def _(pe):
            pe.wait_ge(w_loaded, 16 * n_weights)
            pe.wait_ge(pool_done, B)
            mm(pp[0:AA, 0, 0:B].rearrange("a (h k) -> a h k", k=2), w["fc_wT"][:], pooled.rearrange("p k h -> p h k"),
               start=True, stop=True).then_inc(setup_pe, 1)
            pe.wait_ge(setup_dve, 3)
            mm(pp[:, 0, 0:B], w["ch_wT"][:], h_att, start=True, stop=True).then_inc(setup_pe, 1)
            for b in range(B):
                last = mm(pp[:, 1, 13 * b:13 * b + 13], hrep[:, b, :], w["spke_wT"][:], start=(b == 0), stop=True,
                          skip_group_check=True)
            last.then_inc(setup_pe, 1)

            def conv(b, c, t0, t1):
                taps = [4, 0, 1, 2, 3, 5, 6, 7, 8]
                rows = xin[:, c % 2, :].rearrange("p (r w) -> p r w", w=W)
                acc = pp[:, 0, :].rearrange("p (r w) -> p r w", w=W)
                for n in range(t0, t1):
                    kh, kw = divmod(taps[n], 3)
                    ra, rb = (1 if c % CH == 0 and kh == 0 else 0), (ROWS - 1 if c % CH == CH - 1 and kh == 2 else ROWS)
                    ca, cb = (1 if kw == 0 else 0), (W - 1 if kw == 2 else W)
                    last = mm(acc[:, ra:rb, ca:cb], diag[:, taps[n], :], rows[:, ra + kh:rb + kh, ca + kw - 1:cb + kw - 1],
                              start=(n == 0), stop=(n == TAPS - 1))
                if t1 == TAPS:
                    last.then_inc(conv_done, 1)

            def step_conv(b, c, t0, t1):
                if t0 == 0:
                    pe.wait_ge(x_loaded[c % 2], 16 * (b * (CH // 2) + c // 2 + 1))
                    if c % CH == 0:
                        pe.wait_ge(diag_ready, b + c // CH + 1)
                    if not (isinstance(b, int) and b * CH + c == 0):
                        pe.wait_ge(z_done, b * CH + c)
                conv(b, c, t0, t1)

            def step_y(b, c):
                pe.wait_ge(y_evac, b * CH + c + 1)
                mm(pp[:, 0, :], w["b1T"][:], ysb[:], start=True, stop=True)
                mm(pp[:, 1, :], w["b2T"][:], ysb[:], start=True, stop=True).then_inc(y12_done, 1)

            def step_gc(b, c):
                pe.wait_ge(g_done, b * CH + c + 1)
                mm(pp[:, 0, :], w["center"][:], gbuf[:], start=True, stop=True).then_inc(gc_done, 1)

            def step_var(b, c):
                pe.wait_ge(sq_done, b * CH + c + 1)
                mm(pp[:, 1, :], w["ones"][:], sq[:], start=True, stop=True).then_inc(var_done, 1)

            def step_xh(b, c, d):
                if d == 0:
                    pe.wait_ge(x1_done, b * CH + c + 1)
                mm(pp[:, d, :], W_taps[:, 1, d * P:(d + 1) * P], x1_cols(c), start=True, stop=False)
                mm(pp[:, d, :], W_taps[:, 0, d * P:(d + 1) * P], x1_cols(c, shift=1), start=False,
                   stop=True).then_inc(xh_mm, 1)

            def step_dbl(b, c):
                pe.wait_ge(xh_done, 2 * (b * CH + c + 1))
                for d in range(DI):
                    last = mm(pp[0:NDBL, 0, :], w["Wx"][:, d, :], xh[:, c % 4, d, :], start=(d == 0), stop=(d == 1))
                last.then_inc(dbl_mm, 1)

            def step_bc(b, c):
                pe.wait_ge(dbl_done, b * CH + c + 1)
                for k in range(2):
                    last = mm(pp[:, k, :], w["bcsel"][:, k, :], dbl[0:NDBL + 1, :], start=True, stop=True)
                last.then_inc(bc_mm, 1)

            def step_dt(b, c):
                pe.wait_ge(bc_done, b * CH + c + 1)
                for d in range(DI):
                    last = mm(pp[:, d, :], w["wdt"][:, d * P:(d + 1) * P], dbl[0:NDBL + 1, :], start=True, stop=True)
                last.then_inc(dt_mm, 1)

            def step_z(b, c):
                for d in (1, 0):
                    if d == 1:
                        pe.wait_ge(dt_done, b * CH + c + 1)
                    elif not (isinstance(b, int) and b * CH + c < 2):
                        pe.wait_ge(o_done, b * CH + c - 1)
                    last = mm(pp[:, d, :], w["W_in"][:, (2 + d) * P:(3 + d) * P], x1_cols(c), start=True, stop=True)
                last.then_inc(z_mm, 1)

            def step_out(b, c, alone=False):
                pe.wait_ge(yz_done, b * CH + c + 1)
                if not alone:
                    pe.wait_ge(dt_done, b * CH + c + 3)
                for d in range(DI):
                    last = mm(pp[:, 0, :], w["Wout"][:, d, :], y[:, d, :], start=(d == 0), stop=(d == 1))
                last.then_inc(out_mm, 1)

            def group_sums(b):
                pe.wait_ge(gst_done, b + 1)
                mm(pp[:, 1, 0:2], w["gblock"][:], gst[:], start=True, stop=True).then_inc(gmm_done, 1)

            def broadcast(b, c, i):
                d, j, e = subgroup(i)
                n = (b * CH + c) * SUB + i
                fresh = isinstance(n, int)
                if i == 0:
                    pe.wait_ge(dt_stacked, 192 * (b * CH + c + 1))
                if not fresh or n >= 2:
                    pe.wait_ge(exp_done, n - 1)
                mm(ps_dt[:, i % 2, :], selb[:, e, :], stack["dt"][:, c % 2, 4 * d + j, :], start=True,
                   stop=True).then_inc(dtb_mm, 1)
                if i == 0:
                    pe.wait_ge(dtx_stacked, 192 * (b * CH + c + 1))
                if not fresh or n >= RX:
                    pe.wait_ge(bmul_done, n - last_use(i) + 1)
                mm(ps_x[:, i % RX, :], selb[:, e, :], stack["dtx"][:, c % 2, 4 * d + j, :], start=True,
                   stop=True).then_inc(xb_mm, 1)

            def sum_states(b, c, m):
                q = (b * CH + c) * QUADS + m
                pe.wait_ge(cmul_done, 2 * q + 2)
                if m % 4 == 0 and not (isinstance(q, int) and q == 0):
                    pe.wait_ge(yacc_done, (b * CH + c) * DI + m // 4)
                for k in range(4):
                    last = mm(ps_acc[32 * k:32 * k + 32, :], w["selsum"][:, m % 4, :], hq[:, m % HQ, k, :],
                              start=(m % 4 == 0), stop=(m % 4 == 3))
                last.then_inc(sum_done, 1)

            def chunk(b, c, end):
                for u in range(2 * SLOTS):
                    broadcast(b, c, u)
                    if u % 4 == SUM_LAG % 4:
                        m = (u - SUM_LAG) // 4
                        if m >= 0:
                            sum_states(b, c, m)
                        elif c:
                            sum_states(b, c - 1, m + QUADS)
                    if c and u == PE_OUT:
                        step_out(b, c - 1, alone=c + 1 >= end)
                    if c + 1 < end:
                        for d in range(DI):
                            if u == PE_XH[d]:
                                step_xh(b, c + 1, d)
                        if u == PE_DBL:
                            step_dbl(b, c + 1)
                        if u == PE_BC:
                            step_bc(b, c + 1)
                        if u == PE_DT:
                            step_dt(b, c + 1)
                        if u == PE_Z:
                            step_z(b, c + 1)
                    if c + 2 < end:
                        for k in range(TAPS):
                            if u == PE_CONV[k]:
                                step_conv(b, c + 2, k, k + 1)
                        if u == PE_Y:
                            if c == CH:
                                pe.wait_ge(gmv_done, 3 * b + 1)
                            step_y(b, c + 2)
                        if u == PE_GC:
                            step_gc(b, c + 2)
                        if u == PE_VAR:
                            step_var(b, c + 2)
                    if c == CH and u == 2 * GN_SUM + 1:
                        group_sums(b)

            step_conv(0, 0, 0, TAPS)
            step_y(0, 0)
            step_gc(0, 0)
            step_var(0, 0)
            step_xh(0, 0, 0)
            step_xh(0, 0, 1)
            step_dbl(0, 0)
            step_bc(0, 0)
            step_dt(0, 0)
            step_z(0, 0)
            step_conv(0, 1, 0, TAPS)
            step_y(0, 1)
            step_gc(0, 1)
            step_var(0, 1)
            chunk(0, 0, CH + 3)
            with pe.Fori(0, B - 1, 1) as b:
                for c in range(1, CH + 1):
                    chunk(b, c, CH + 3)
            for c in range(1, CH):
                chunk(B - 1, c, CH)
            sum_states(B - 1, CH - 1, QUADS - 2)
            sum_states(B - 1, CH - 1, QUADS - 1)
            pe.wait_ge(o_done, B * CH - 1)
            step_out(B - 1, CH - 1, alone=True)
            group_sums(B - 1)

        @block.scalar
        def _(act):
            A = nc.scalar.activation
            act.wait_ge(w_loaded, 16 * n_weights)
            act.wait_ge(consts_ready, 4)
            with act.Fori(0, B // 2, 1) as h:
                for k in range(2):
                    act.wait_ge(xpool_loaded[k], 16 * h + 16)
                    A(xp[k], xp[k], ACT.Identity, scale=1.0 / L, accum_out=pooled[:, k, bass.ds(h, 1)]).then_inc(pool_done, 1)
            A(bn_s[:, 0:1], w["bn"][:, 3:4], ACT.Ln, bias=eps[0:AA, 0:1]).then_inc(setup_act, 1)
            act.wait_ge(setup_act, 1)
            A(bn_s[:, 1:2], bn_s[:, 0:1], ACT.Exp, scale=-0.5).then_inc(setup_act, 1)
            A(A_neg[:], w["A_log"][:], ACT.Exp).then_inc(setup_act, 1)
            act.wait_ge(setup_dve, 4)
            A(spke[:, :, 9:13], spke[:, :, 9:13], ACT.Exp).then_inc(setup_act, 1)
            act.wait_ge(setup_pe, 3)
            A(ch_att, pp[:, 0, 0:B], ACT.Sigmoid, bias=w["ch_b"][:]).then_inc(setup_act, 1)
            A(spke[:, :, 0:9], spke[:, :, 0:9], ACT.Sigmoid).then_inc(setup_act, 1)

            def evac_conv(b, c):
                act.wait_ge(conv_done, b * CH + c + 1)
                A(ysb[:], pp[:, 0, :], ACT.Copy).then_inc(y_evac, 1)

            def gelu(b, c):
                act.wait_ge(y12_done, b * CH + c + 1)
                A(gbuf[:], pp[:, 0, :], ACT.Gelu, bias=w["vec0"][:, 0:1]).then_inc(gelu_done, 1)

            def square(b, c):
                act.wait_ge(gc_done, b * CH + c + 1)
                A(sq[:], pp[:, 0, :], ACT.Square).then_inc(sq_done, 1)

            def rstd(b, c):
                act.wait_ge(var_done, b * CH + c + 1)
                A(sq[:], pp[:, 1, :], ACT.Ln, bias=eps[:, 1:2]).then_inc(lnv_done, 1)
                act.wait_ge(lnv_done, b * CH + c + 1)
                A(sq[:], sq[:], ACT.Exp, scale=-0.5).then_inc(rstd_done, 1)

            def silu_xh(b, c, d):
                act.wait_ge(xh_mm, 2 * (b * CH + c) + d + 1)
                A(xh[:, c % 4, d, :], pp[:, d, :], ACT.Silu, bias=w["cb"][:, d:d + 1]).then_inc(xh_done, 1)

            def evac_dbl(b, c):
                act.wait_ge(dbl_mm, b * CH + c + 1)
                A(dbl[0:NDBL, :], pp[0:NDBL, 0, :], ACT.Copy).then_inc(dbl_done, 1)

            def evac_bc(b, c):
                act.wait_ge(bc_mm, b * CH + c + 1)
                A(bc[:, c % 2, :, :], pp[:, :, :], ACT.Copy).then_inc(bc_done, 1)

            def softplus_tail(b, c, k):
                if k == 0:
                    act.wait_ge(dt_mm, b * CH + c + 1)
                    A(sp[:], pp[:, :, :], ACT.Abs).then_inc(sp_done, 1)
                else:
                    act.wait_ge(sp_done, 3 * (b * CH + c) + k)
                    if k == 1:
                        A(sp[:], sp[:], ACT.Exp, scale=-1.0).then_inc(sp_done, 1)
                    else:
                        A(sp[:], sp[:], ACT.Ln, bias=1.0).then_inc(sp_done, 1)

            def cast_part(b, c, n, k):
                src, ready, done = {("dt", 0): (dt, dt_done, dthi_done), ("dt", 1): (res, dtres_done, dtmid_done),
                                    ("dtx", 0): (dtx, dtx_done, dtxhi_done), ("dtx", 1): (res, dtxres_done, dtxmid_done)}[n, k]
                act.wait_ge(ready, b * CH + c + 1)
                A(parts[n][k][:], src[:], ACT.Copy).then_inc(done, 1)

            def silu_z(b, c):
                act.wait_ge(z_mm, b * CH + c + 1)
                A(sz[:, c % 2, :, :], pp[:, :, :], ACT.Silu).then_inc(z_done, 1)

            def evac_out(b, c):
                act.wait_ge(out_mm, b * CH + c + 1)
                if c == 0:
                    act.wait_ge(stored, 64 * b + 16)
                A(o[:, c * T:(c + 1) * T], pp[:, 0, :], ACT.Identity, accum_out=osum[:, 0, c:c + 1])
                A(y[:, 0, :], pp[:, 0, :], ACT.Square, accum_out=osum[:, 1, c:c + 1]).then_inc(o_done, 1)

            def decay(b, c, i):
                n = (b * CH + c) * SUB + i
                act.wait_ge(dtb_mm, n + 1)
                if not (isinstance(n, int) and n < RD):
                    act.wait_ge(scan_done, n - RD + 1)
                A(dA[:, i % RD, :], ps_dt[:, i % 2, :], ACT.Exp, scale=A_neg[:, i:i + 1]).then_inc(exp_done, 1)

            def group_rstd(b):
                act.wait_ge(gmv_done, 3 * b + 3)
                A(gmv[:, 2:3], gmv[:, 2:3], ACT.Ln, bias=eps[:, 2:3]).then_inc(grs_done, 1)
                act.wait_ge(grs_done, 2 * b + 1)
                A(gmv[:, 3:4], gmv[:, 2:3], ACT.Exp, scale=-0.5).then_inc(grs_done, 1)

            def group_silu(b):
                act.wait_ge(gsc_done, 3 * b + 3)
                for k in range(4):
                    piece = o[:, k * (L // 4):(k + 1) * (L // 4)]
                    A(piece, piece, ACT.Silu, scale=gmv[:, 4:5], bias=gmv[:, 5:6]).then_inc(silu_done, 1)
                act.preload_act_table_set(LN_EXP)

            def chunk(b, c, end):
                for u in range(2 * SLOTS):
                    decay(b, c, u)
                    if c and u == ACT_OUT:
                        evac_out(b, c - 1)
                    if c + 1 < end:
                        if u == ACT_XH:
                            silu_xh(b, c + 1, 0)
                            silu_xh(b, c + 1, 1)
                            act.preload_act_table_set(LN_EXP)
                        if u == ACT_DBL:
                            evac_dbl(b, c + 1)
                        if u == ACT_BC:
                            evac_bc(b, c + 1)
                        for k in range(3):
                            if u == ACT_SP[k]:
                                softplus_tail(b, c + 1, k)
                        if u == ACT_DTHI:
                            cast_part(b, c + 1, "dt", 0)
                        if u == ACT_Z:
                            silu_z(b, c + 1)
                            act.preload_act_table_set(LN_EXP)
                        if u == ACT_DTMID:
                            cast_part(b, c + 1, "dt", 1)
                        if u == ACT_DTXHI:
                            cast_part(b, c + 1, "dtx", 0)
                        if u == ACT_DTXMID:
                            cast_part(b, c + 1, "dtx", 1)
                    if c + 2 < end:
                        if u == ACT_CONV:
                            evac_conv(b, c + 2)
                        if u == ACT_GELU:
                            gelu(b, c + 2)
                            act.preload_act_table_set(LN_EXP)
                        if u == ACT_SQ:
                            square(b, c + 2)
                        if u == ACT_RSTD:
                            rstd(b, c + 2)
                    if c == CH and u == 2 * GN_SUM + 3:
                        group_rstd(b)
                    if c == CH and u == 2 * GN_SUM + 7:
                        group_silu(b)

            act.wait_ge(batch_done, 1)
            act.preload_act_table_set(LN_EXP)
            evac_conv(0, 0)
            gelu(0, 0)
            act.preload_act_table_set(LN_EXP)
            square(0, 0)
            rstd(0, 0)
            silu_xh(0, 0, 0)
            silu_xh(0, 0, 1)
            act.preload_act_table_set(LN_EXP)
            evac_dbl(0, 0)
            evac_bc(0, 0)
            for k in range(3):
                softplus_tail(0, 0, k)
            cast_part(0, 0, "dt", 0)
            cast_part(0, 0, "dt", 1)
            silu_z(0, 0)
            cast_part(0, 0, "dtx", 0)
            cast_part(0, 0, "dtx", 1)
            evac_conv(0, 1)
            gelu(0, 1)
            act.preload_act_table_set(LN_EXP)
            square(0, 1)
            rstd(0, 1)
            chunk(0, 0, CH + 3)
            with act.Fori(0, B - 1, 1) as b:
                for c in range(1, CH + 1):
                    chunk(b, c, CH + 3)
            for c in range(1, CH):
                chunk(B - 1, c, CH)
            evac_out(B - 1, CH - 1)
            group_rstd(B - 1)
            group_silu(B - 1)

        @block.vector
        def _(dve):
            v = nc.vector
            for k, e in enumerate((BN_EPS, LN_EPS, GN_EPS)):
                v.memset(eps[:, k:k + 1], e).then_inc(consts_ready, 1)
            v.memset(dbl[:], 1.0).then_inc(consts_ready, 1)
            v.memset(bn_s[:, 3:4], 0.0).then_inc(stored, 16)
            v.memset(x1n[:, 0:1], 0.0)
            dve.wait_ge(w_loaded, 16 * n_weights)
            v.tensor_copy(selb[:].rearrange("r e k -> r (e k)"), dA[0:96, 0, :])
            dve.wait_ge(setup_act, 2)
            dve.wait_ge(setup_pe, 1)
            v.tensor_tensor(bn_s[:, 2:3], bn_s[:, 1:2], w["bn"][:, 0:1], ALU.mult).then_inc(setup_dve, 1)
            dve.wait_ge(setup_dve, 1)
            v.tensor_scalar(h_att, pp[0:AA, 0, 0:B], w["bn"][:, 2:3], bn_s[:, 2:3], ALU.subtract, ALU.mult).then_inc(setup_dve, 1)
            dve.wait_ge(setup_dve, 2)
            v.tensor_scalar(h_att, h_att, w["bn"][:, 1:2], 0.0, ALU.add, ALU.max).then_inc(t_done, 1)
            dve.wait_ge(t_done, 1)
            v.tensor_copy(hrep, h_att.unsqueeze(2).to_broadcast([AA, B, P])).then_inc(setup_dve, 1)
            dve.wait_ge(setup_pe, 3)
            v.tensor_tensor(spke, pp[:, 1, 0:13 * B].rearrange("p (b k) -> p b k", b=B),
                            w["spke_b"][:].unsqueeze(1).to_broadcast([P, B, 13]), ALU.add).then_inc(t_done, 1)
            dve.wait_ge(t_done, 2)
            v.tensor_reduce(kmx.unsqueeze(2), spke[:, :, 9:13], AX.X, ALU.max).then_inc(t_done, 1)
            dve.wait_ge(t_done, 3)
            v.tensor_tensor(spke[:, :, 9:13], spke[:, :, 9:13], kmx.unsqueeze(2).to_broadcast([P, B, KK]),
                            ALU.subtract).then_inc(setup_dve, 1)
            dve.wait_ge(setup_act, 6)
            v.tensor_reduce(kmx.unsqueeze(2), spke[:, :, 9:13], AX.X, ALU.add).then_inc(t_done, 1)
            dve.wait_ge(t_done, 4)
            v.reciprocal(kmx, kmx).then_inc(t_done, 1)
            dve.wait_ge(t_done, 5)
            v.tensor_tensor(kmx, kmx, ch_att, ALU.mult).then_inc(t_done, 1)
            n = 6
            for k in range(KK):
                dst = wts[:] if k == 0 else od_t
                dve.wait_ge(t_done, n)
                v.tensor_tensor(dst, w["od"][:, k, :].unsqueeze(1).to_broadcast([P, B, TAPS]),
                                spke[:, :, 9 + k:10 + k].to_broadcast([P, B, TAPS]), ALU.mult).then_inc(t_done, 1)
                n += 1
                if k:
                    dve.wait_ge(t_done, n)
                    v.tensor_tensor(wts[:], wts[:], od_t, ALU.add).then_inc(t_done, 1)
                    n += 1
            dve.wait_ge(t_done, n)
            v.tensor_tensor(wts[:], wts[:], spke[:, :, 0:9], ALU.mult).then_inc(t_done, 1)
            dve.wait_ge(t_done, n + 1)
            v.tensor_tensor(wts[:], wts[:], kmx.unsqueeze(2).to_broadcast([P, B, TAPS]), ALU.mult).then_inc(t_done, 1)
            setup_t = n + 2
            v.tensor_scalar(A_neg[:], A_neg[:], -1.0, None, ALU.mult)
            for k in range(2):
                v.tensor_tensor(W_taps[:, k, :], w["W_in"][:, 0:2 * P], w["cw_rows"][:, k, :], ALU.mult)
            v.memset(x1[:, 0:1], 0.0).then_inc(batch_done, 1)
            dve.wait_ge(t_done, setup_t)
            dve.wait_ge(batch_done, 1)

            def gate(b, c):
                dve.wait_ge(gelu_done, b * CH + c + 1)
                v.scalar_tensor_tensor(gbuf[:], pp[:, 1, :], w["vec0"][:, 1:2], gbuf[:], ALU.add, ALU.mult).then_inc(g_done, 1)

            def norm(b, c):
                dve.wait_ge(rstd_done, b * CH + c + 1)
                v.scalar_tensor_tensor(gbuf[:], pp[:, 0, :], w["vec0"][:, 2:3], sq[:], ALU.mult, ALU.mult).then_inc(t2_done, 1)

            def add_input(b, c):
                dve.wait_ge(t2_done, b * CH + c + 1)
                v.scalar_tensor_tensor(x1_cols(c), gbuf[:], w["vec0"][:, 3:4],
                                       xin[:, c % 2, W:W + T], ALU.add, ALU.add).then_inc(x1_done, 1)

            def softplus(b, c):
                dve.wait_ge(sp_done, 3 * (b * CH + c + 1))
                v.scalar_tensor_tensor(dt[:], pp[:, :, :], 0.0, sp[:], ALU.max, ALU.add).then_inc(dt_done, 1)

            def dt_rest(b, c):
                dve.wait_ge(dthi_done, b * CH + c + 1)
                v.tensor_tensor(res[:], dt[:], parts["dt"][0][:], ALU.subtract).then_inc(dtres_done, 1)

            def dtx_low(b, c):
                dve.wait_ge(dtxmid_done, b * CH + c + 1)
                v.tensor_tensor(parts["dtx"][2][:], res[:], parts["dtx"][1][:], ALU.subtract).then_inc(dtxlo_done, 1)

            def y_acc(b, c, d):
                dve.wait_ge(sum_done, b * CH * QUADS + c * QUADS + 4 * (d + 1))
                if d == 0 and not (isinstance(b, int) and b * CH + c == 0):
                    dve.wait_ge(o_done, b * CH + c)
                v.scalar_tensor_tensor(y[:, d, :], xh[:, c % 4, d, :], w["Dv"][:, d:d + 1], ps_acc[:], ALU.mult,
                                       ALU.add).then_inc(yacc_done, 1)

            def y_gate(b, c):
                dve.wait_ge(yacc_done, 2 * (b * CH + c + 1))
                dve.wait_ge(z_done, b * CH + c + 1)
                v.tensor_tensor(y[:], y[:], sz[:, c % 2, :, :], ALU.mult).then_inc(yz_done, 1)

            def weigh_inputs(b, c, u):
                fresh = isinstance(b, int) and b * CH + c == 0
                for i in (2 * u, 2 * u + 1):
                    n = (b * CH + c) * SUB + i
                    if i == 0:
                        dve.wait_ge(bc_done, b * CH + c + 1)
                    dve.wait_ge(xb_mm, n + 1)
                    if not (fresh and i < RD):
                        dve.wait_ge(scan_done, n - RD + 1)
                    v.tensor_tensor(dbx[:, i % RD, :], ps_x[:, i % RX, :], bc[:, c % 2, 0, :], ALU.mult).then_inc(bmul_done, 1)

            def scan(b, c, u):
                fresh = isinstance(b, int) and b * CH + c == 0
                for i in (2 * u, 2 * u + 1):
                    n = (b * CH + c) * SUB + i
                    m = i // 4
                    dve.wait_ge(bmul_done, n + 1)
                    dve.wait_ge(exp_done, n + 1)
                    if i % 4 == 0 and not (fresh and m < HQ):
                        dve.wait_ge(sum_done, (b * CH + c) * QUADS + m - HQ + 1)
                    if c % CH:
                        dve.wait_ge(carry_done, (b * CH + c - 1) * SLOTS + u + 1)
                    v.tensor_tensor_scan(hq[:, m % HQ, i % 4, :], dA[:, i % RD, :], dbx[:, i % RD, :],
                                         carry[:, i:i + 1] if c % CH else 0.0, ALU.mult, ALU.add).then_inc(scan_done, 1)

            def make_diag(b):
                v.tensor_tensor(diag[:], w["ident"][:].unsqueeze(1).to_broadcast([P, TAPS, P]),
                                wts[:, bass.ds(b, 1), :].rearrange("p o k -> p (o k)").unsqueeze(2).to_broadcast([P, TAPS, P]),
                                ALU.mult).then_inc(diag_ready, 1)

            def group_stats(b):
                dve.wait_ge(o_done, b * CH + CH)
                v.tensor_reduce(gst[:].unsqueeze(2), osum[:], AX.X, ALU.add).then_inc(gst_done, 1)

            def group_moments(b):
                dve.wait_ge(gmm_done, b + 1)
                v.tensor_copy(gmv[:, 0:2], pp[:, 1, 0:2]).then_inc(gmv_done, 1)
                dve.wait_ge(gmv_done, 3 * b + 1)
                v.scalar_tensor_tensor(gmv[:, 2:3], gmv[:, 0:1], gmv[:, 0:1], gmv[:, 1:2], ALU.mult,
                                       ALU.subtract).then_inc(gmv_done, 1)
                dve.wait_ge(gmv_done, 3 * b + 2)
                v.tensor_scalar(gmv[:, 2:3], gmv[:, 2:3], -1.0, 0.0, ALU.mult, ALU.max).then_inc(gmv_done, 1)

            def group_scale(b):
                dve.wait_ge(grs_done, 2 * b + 2)
                v.tensor_tensor(gmv[:, 4:5], gmv[:, 3:4], w["gn"][:, 0:1], ALU.mult).then_inc(gsc_done, 1)
                dve.wait_ge(gsc_done, 3 * b + 1)
                v.tensor_tensor(gmv[:, 5:6], gmv[:, 0:1], gmv[:, 4:5], ALU.mult).then_inc(gsc_done, 1)
                dve.wait_ge(gsc_done, 3 * b + 2)
                v.tensor_tensor(gmv[:, 5:6], w["gn"][:, 1:2], gmv[:, 5:6], ALU.subtract).then_inc(gsc_done, 1)

            def add_residual(b, k):
                s = slice(k * (L // 4), (k + 1) * (L // 4))
                dve.wait_ge(silu_done, 4 * b + k + 1)
                v.tensor_tensor(o[:, s], o[:, s], x1[:, 1 + s.start:1 + s.stop], ALU.add).then_inc(fin_done, 1)

            def keep_next(done):
                if done is not None:
                    dve.wait_ge(fin_done, done)
                v.tensor_copy(x1[:, 1:1 + 2 * T], x1n[:, 1:1 + 2 * T])

            def chunk(b, c, end):
                for u in range(2 * SLOTS):
                    if u % 2 == 0:
                        weigh_inputs(b, c, u // 2)
                    else:
                        scan(b, c, u // 2)
                    if c and u == DVE_Y1:
                        y_acc(b, c - 1, 1)
                    if c and u == DVE_YZ:
                        y_gate(b, c - 1)
                    if u == DVE_Y0:
                        y_acc(b, c, 0)
                    if c + 1 < end:
                        if u == DVE_NORM[0]:
                            norm(b, c + 1)
                        if u == DVE_NORM[1]:
                            add_input(b, c + 1)
                        if u == DVE_DT:
                            softplus(b, c + 1)
                        if u == DVE_DTREST:
                            dt_rest(b, c + 1)
                        if u == DVE_DTXLOW:
                            dtx_low(b, c + 1)
                    if c + 2 < end:
                        if u == DVE_GATE:
                            gate(b, c + 2)
                        if c == CH - 2 and u == 11:
                            dve.wait_ge(conv_done, b * CH + CH)
                            make_diag(b + 1)
                    if c == CH:
                        if u == 2 * GN_SUM - 1:
                            group_stats(b)
                        if u == 2 * GN_SUM + 1:
                            group_moments(b)
                        if u == 2 * GN_SUM + 5:
                            group_scale(b)
                        if u == 2 * GN_SUM + 9:
                            add_residual(b, 0)
                            add_residual(b, 1)
                        if u == 2 * GN_SUM + 11:
                            add_residual(b, 2)
                            add_residual(b, 3)
                            keep_next(4 * b + 4)

            make_diag(0)
            gate(0, 0)
            norm(0, 0)
            add_input(0, 0)
            softplus(0, 0)
            dt_rest(0, 0)
            dtx_low(0, 0)
            gate(0, 1)
            chunk(0, 0, CH + 3)
            keep_next(None)
            with dve.Fori(0, B - 1, 1) as b:
                for c in range(1, CH + 1):
                    chunk(b, c, CH + 3)
            for c in range(1, CH):
                chunk(B - 1, c, CH)
            y_acc(B - 1, CH - 1, 1)
            y_gate(B - 1, CH - 1)
            group_stats(B - 1)
            group_moments(B - 1)
            group_scale(B - 1)
            for k in range(4):
                add_residual(B - 1, k)

        @block.gpsimd
        def _(pool):
            g = nc.gpsimd

            def dt_low(b, c):
                pool.wait_ge(dtmid_done, b * CH + c + 1)
                g.tensor_tensor(parts["dt"][2][:], res[:], parts["dt"][1][:], ALU.subtract).then_inc(dtlo_done, 1)

            def dt_x(b, c):
                pool.wait_ge(dtres_done, b * CH + c + 1)
                pool.wait_ge(xh_done, 2 * (b * CH + c + 1))
                g.tensor_tensor(dtx[:], dt[:], xh[:, c % 4, :, :], ALU.mult).then_inc(dtx_done, 1)

            def dtx_rest(b, c):
                pool.wait_ge(dtxhi_done, b * CH + c + 1)
                pool.wait_ge(dtlo_done, b * CH + c + 1)
                g.tensor_tensor(res[:], dtx[:], parts["dtx"][0][:], ALU.subtract).then_inc(dtxres_done, 1)

            def weigh_states(b, c, u):
                n = (b * CH + c) * SLOTS + u
                pair = hq[:, (u // 2) % HQ, 2 * (u % 2):2 * (u % 2) + 2, :]
                pool.wait_ge(scan_done, 2 * n + 2)
                pool.sem_inc(pair_seen, 1)
                g.tensor_copy(carry[:, 2 * u:2 * u + 2].unsqueeze(2), pair[:, :, T - 1:T]).then_inc(carry_done, 1)
                pool.wait_ge(carry_done, n + 1)
                g.tensor_tensor(pair, pair, bc[:, c % 2, 1, :].unsqueeze(1).to_broadcast([P, 2, T]),
                                ALU.mult).then_inc(cmul_done, 1)

            def chunk(b, c, end):
                for u in range(SLOTS):
                    weigh_states(b, c, u)
                    if c + 1 < end:
                        if u == POOL_DTX:
                            dt_x(b, c + 1)
                        if u == POOL_DTLOW:
                            dt_low(b, c + 1)
                        if u == POOL_DTXREST:
                            dtx_rest(b, c + 1)

            pool.wait_ge(batch_done, 1)
            dt_x(0, 0)
            dt_low(0, 0)
            dtx_rest(0, 0)
            chunk(0, 0, CH + 3)
            with pool.Fori(0, B - 1, 1) as b:
                for c in range(1, CH + 1):
                    chunk(b, c, CH + 3)
            for c in range(1, CH):
                chunk(B - 1, c, CH)


def _layout(i):
    f = lambda n: np.asarray(i[n])
    c = np.ascontiguousarray
    a = {"x": f("x")}
    a["fc_wT"] = f("L0_conv_fc_w").T
    a["bn"] = np.stack([f("L0_conv_bn_gamma"), f("L0_conv_bn_beta"), f("L0_conv_bn_mean"), f("L0_conv_bn_var")], 1)
    a["ch_wT"] = f("L0_conv_ch_w").T
    a["ch_b"] = f("L0_conv_ch_b")[:, None]
    a["spke_wT"] = np.concatenate([f("L0_conv_sp_w"), f("L0_conv_ke_w")], 0).T
    a["spke_b"] = np.repeat(np.concatenate([f("L0_conv_sp_b"), f("L0_conv_ke_b")])[None], P, 0)
    a["od"] = f("L0_conv_od_weight").reshape(KK, P, TAPS).transpose(1, 0, 2)
    a["b1T"] = f("L0_conv_b1_w").T
    a["b2T"] = f("L0_conv_b2_w").T
    a["vec0"] = np.stack([f("L0_conv_b1_b"), f("L0_conv_b2_b"), f("L0_conv_ln_w"), f("L0_conv_ln_b")], 1)
    a["W_in"] = f("L1_conv_W_in")
    a["cw_rows"] = np.repeat(f("L1_conv_conv_w").T[None], P, 0)
    a["cb"] = f("L1_conv_conv_b").reshape(DI, P).T
    a["Wx"] = f("L1_conv_W_x").reshape(DI, P, NDBL).transpose(1, 0, 2)
    wdt = np.zeros((NDBL + 1, 2 * P), np.float32)
    wdt[0:R] = f("L1_conv_W_dt")
    wdt[NDBL] = f("L1_conv_b_dt")
    a["wdt"] = wdt
    al = f("L1_conv_A_log").reshape(DI, 4, 4, P)
    a["A_log"] = np.stack([al[d, j, e] for d, j, e in map(subgroup, range(SUB))], 1)
    a["Dv"] = f("L1_conv_D").reshape(DI, P).T
    a["Wout"] = f("L1_conv_W_out").reshape(DI, P, P).transpose(1, 0, 2)
    a["gn"] = np.stack([f("L1_conv_gn_gamma"), f("L1_conv_gn_beta")], 1)
    a["ident"] = np.eye(P, dtype=np.float32)
    a["center"] = np.eye(P, dtype=np.float32) - np.float32(1 / P)
    a["ones"] = np.full((P, P), 1 / P, np.float32)
    a["gblock"] = np.kron(np.eye(GROUPS), np.full((P // GROUPS,) * 2, GROUPS / P / L)).astype(np.float32)
    part = np.arange(P)
    bcsel = np.zeros((NDBL + 1, 2, P), np.float32)
    for k in range(2):
        bcsel[R + NS * k + part % NS, k, part] = 1
    a["bcsel"] = bcsel
    selsum = np.zeros((P, 4, 32), np.float32)
    selb = np.zeros((96, 4, P), np.float32)
    for e in range(4):
        selsum[part, e, DSUB * e + part // NS] = 1
        for k in range(3):
            selb[32 * k + DSUB * e + part // NS, e, part] = 1
    a["selsum"], a["selb"] = selsum, selb
    return {k: c(v) for k, v in a.items()}


def kernel(**inputs):
    import concourse.bacc as _bacc
    from concourse.bass_utils import run_bass_kernel_spmd as _run

    arrays = _layout(inputs)
    nc = _bacc.Bacc("TRN2", target_bir_lowering=False, num_devices=1)
    args = {n: nc.dram_tensor(f"in_{n}", v.shape, mybir.dt.from_np(v.dtype), kind="ExternalInput").ap()
            for n, v in arrays.items()}
    out = nc.dram_tensor("out", arrays["x"].shape, F32, kind="ExternalOutput").ap()
    build_program(nc, args, out)
    r = _run(nc, [{f"in_{n}": v for n, v in arrays.items()}], core_ids=[0])
    return r.results[0]["out"]
```
